# Optimizing a Trainium2 kernel written in Bass

```python
import numpy as np
import jax
import jax.numpy as jnp

def _softmax(x, axis=-1):
    return jax.nn.softmax(x, axis=axis)

def _gelu(x):
    return jax.nn.gelu(x, approximate=True)

def _silu(x):
    return jax.nn.silu(x)

def _sigmoid(x):
    return jax.nn.sigmoid(x)

def _layernorm(x, axis=-1, eps=1e-05):
    m = jnp.mean(x, axis=axis, keepdims=True)
    v = jnp.var(x, axis=axis, keepdims=True)
    return (x - m) / jnp.sqrt(v + eps)

def _scatter_add(tgt, idx, src, axis=0):
    return tgt.at[idx].add(src)

def _segment_sum(src, seg, n):
    return jax.ops.segment_sum(src, seg, n)
kernel_name = 'mk_gnn_preln_d2_gnn_r32_af7b15'

def setup_inputs(seed: int=0):
    np.random.seed(seed)
    _w = jnp.asarray

    def _rec_inputs():
        import jax
        import jax.numpy as jnp
        _gk = jax.random.key(seed)
        x = -0.0002117 + 1 * jax.random.normal(jax.random.fold_in(_gk, 1), (3125, 256), jnp.float32)
        _s = jax.random.randint(jax.random.fold_in(_gk, 2), (25000,), 0, 3125, jnp.int32)
        _d = jax.random.randint(jax.random.fold_in(_gk, 3), (25000,), 0, 3125, jnp.int32)
        _loop = jnp.arange(3125, dtype=jnp.int32)
        src = jnp.concatenate([_s, _d, _loop])
        dst = jnp.concatenate([_d, _s, _loop])
        _o = jnp.argsort(dst, stable=True)
        src = src[_o]
        dst = dst[_o]
        edge_type_2 = jax.random.randint(jax.random.fold_in(_gk, 13), (53125,), 0, 2, jnp.int32)
        edge_weight = jax.random.uniform(jax.random.fold_in(_gk, 14), (53125,), jnp.float32, 0.0, 1)
        return (x, src, dst, edge_type_2, edge_weight)
    x, src, dst, edge_type_2, edge_weight = _rec_inputs()

    def _L0_gnn_setup():
        import jax, jax.numpy as jnp
        import numpy as np
        BN_EPS = 1e-05

        def _batchnorm(h, gamma, beta):
            mean = jnp.mean(h, axis=0, keepdims=True)
            var = jnp.var(h, axis=0, keepdims=True)
            return (h - mean) * jax.lax.rsqrt(var + BN_EPS) * gamma + beta
        key = jax.random.key(seed)
        ks = jax.random.split(key, 10)
        N, E, D = (3125, 100000, 256)
        x = jax.random.normal(ks[0], (N, D), dtype=jnp.float32)
        edge_src = jax.random.randint(ks[1], (E,), 0, N, dtype=jnp.int32)
        edge_dst = jax.random.randint(ks[2], (E,), 0, N, dtype=jnp.int32)
        edge_vals = jnp.ones((E,), dtype=jnp.float32)
        n_norm = jax.random.uniform(ks[3], (N, 1), dtype=jnp.float32)
        s = 1.0 / np.sqrt(D)
        w1 = jax.random.uniform(ks[4], (D, D), jnp.float32, -s, s)
        gamma1 = jnp.ones((D,), jnp.float32)
        beta1 = jnp.zeros((D,), jnp.float32)
        w2 = jax.random.uniform(ks[5], (D, D), jnp.float32, -s, s)
        eps_weight = jnp.zeros((1,), jnp.float32)
        gamma_h = jnp.ones((D,), jnp.float32)
        beta_h = jnp.zeros((D,), jnp.float32)
        return {'x': x, 'edge_src': edge_src, 'edge_dst': edge_dst, 'edge_vals': edge_vals, 'n_norm': n_norm, 'w1': w1, 'gamma1': gamma1, 'beta1': beta1, 'w2': w2, 'eps_weight': eps_weight, 'gamma_h': gamma_h, 'beta_h': beta_h}
    _L0_gnn_all = _L0_gnn_setup()
    _L0_gnn_in = {k: v for k, v in _L0_gnn_all.items() if k in ('w1', 'gamma1', 'beta1', 'w2', 'eps_weight', 'gamma_h', 'beta_h')}
    del _L0_gnn_all

    def _L1_gnn_setup():
        import jax, jax.numpy as jnp
        import numpy as np
        N_NODES = 10000
        N_EDGES = 10000
        D = 256
        D_OUT = 256
        NUM_REL = 2
        key = jax.random.key(seed)
        ks = jax.random.split(key, 16)
        s = 1.0 / np.sqrt(D)
        inp = {}
        inp['feat'] = jax.random.normal(ks[0], (N_NODES, D), dtype=jnp.float32)
        inp['src'] = jax.random.randint(ks[1], (N_EDGES,), 0, N_NODES, dtype=jnp.int32)
        inp['dst'] = jax.random.randint(ks[2], (N_EDGES,), 0, N_NODES, dtype=jnp.int32)
        inp['rel'] = jax.random.randint(ks[3], (N_EDGES,), 0, NUM_REL, dtype=jnp.int32)
        inp['W_rel'] = jax.random.normal(ks[4], (NUM_REL, D, D), dtype=jnp.float32) * s
        inp['b_rel'] = jax.random.normal(ks[5], (NUM_REL, D), dtype=jnp.float32) * s
        inp['W_ih'] = jax.random.normal(ks[6], (4 * D, D), dtype=jnp.float32) * s
        inp['b_ih'] = jax.random.normal(ks[7], (4 * D,), dtype=jnp.float32) * s
        inp['b_hh'] = jax.random.normal(ks[8], (4 * D,), dtype=jnp.float32) * s
        h = D // 2
        inp['W1'] = jax.random.normal(ks[9], (h, D), dtype=jnp.float32) * s
        inp['b1'] = jax.random.normal(ks[10], (h,), dtype=jnp.float32) * s
        inp['W2'] = jax.random.normal(ks[11], (h, h), dtype=jnp.float32) * (1.0 / np.sqrt(h))
        inp['b2'] = jax.random.normal(ks[12], (h,), dtype=jnp.float32) * (1.0 / np.sqrt(h))
        inp['W3'] = jax.random.normal(ks[13], (D_OUT, h), dtype=jnp.float32) * (1.0 / np.sqrt(h))
        inp['b3'] = jax.random.normal(ks[14], (D_OUT,), dtype=jnp.float32) * (1.0 / np.sqrt(h))
        return inp
    _L1_gnn_all = _L1_gnn_setup()
    _L1_gnn_in = {k: v for k, v in _L1_gnn_all.items() if k in ('W_rel', 'b_rel', 'W_ih', 'b_ih', 'b_hh', 'W1', 'b1', 'W2', 'b2', 'W3', 'b3')}
    del _L1_gnn_all
    return {'x': x, 'src': src, 'dst': dst, 'edge_type_2': edge_type_2, 'edge_weight': edge_weight, 'L0_gnn_w1': _L0_gnn_in['w1'], 'L0_gnn_gamma1': _L0_gnn_in['gamma1'], 'L0_gnn_beta1': _L0_gnn_in['beta1'], 'L0_gnn_w2': _L0_gnn_in['w2'], 'L0_gnn_eps_weight': _L0_gnn_in['eps_weight'], 'L0_gnn_gamma_h': _L0_gnn_in['gamma_h'], 'L0_gnn_beta_h': _L0_gnn_in['beta_h'], 'L1_gnn_W_rel': _L1_gnn_in['W_rel'], 'L1_gnn_b_rel': _L1_gnn_in['b_rel'], 'L1_gnn_W_ih': _L1_gnn_in['W_ih'], 'L1_gnn_b_ih': _L1_gnn_in['b_ih'], 'L1_gnn_b_hh': _L1_gnn_in['b_hh'], 'L1_gnn_W1': _L1_gnn_in['W1'], 'L1_gnn_b1': _L1_gnn_in['b1'], 'L1_gnn_W2': _L1_gnn_in['W2'], 'L1_gnn_b2': _L1_gnn_in['b2'], 'L1_gnn_W3': _L1_gnn_in['W3'], 'L1_gnn_b3': _L1_gnn_in['b3']}

def reference(x, src, dst, edge_type_2, edge_weight, L0_gnn_w1, L0_gnn_gamma1, L0_gnn_beta1, L0_gnn_w2, L0_gnn_eps_weight, L0_gnn_gamma_h, L0_gnn_beta_h, L1_gnn_W_rel, L1_gnn_b_rel, L1_gnn_W_ih, L1_gnn_b_ih, L1_gnn_b_hh, L1_gnn_W1, L1_gnn_b1, L1_gnn_W2, L1_gnn_b2, L1_gnn_W3, L1_gnn_b3):
    import jax
    import jax.numpy as jnp

    def _L0_gnn_ref(x, edge_src, edge_dst, edge_vals, n_norm, w1, gamma1, beta1, w2, eps_weight, gamma_h, beta_h):
        import jax, jax.numpy as jnp
        import numpy as np
        BN_EPS = 1e-05

        def _batchnorm(h, gamma, beta):
            mean = jnp.mean(h, axis=0, keepdims=True)
            var = jnp.var(h, axis=0, keepdims=True)
            return (h - mean) * jax.lax.rsqrt(var + BN_EPS) * gamma + beta
        N = x.shape[0]
        msgs = edge_vals[:, None] * x[edge_src]
        agg = jax.ops.segment_sum(msgs, edge_dst, num_segments=N)
        y = agg + eps_weight * x
        h = jax.nn.relu(_batchnorm(y @ w1.T, gamma1, beta1))
        y = h @ w2.T
        y = y * n_norm
        y = _batchnorm(y, gamma_h, beta_h)
        y = jax.nn.relu(y)
        y = y + x
        return y

    def _L1_gnn_ref(feat, src, dst, rel, W_rel, b_rel, W_ih, b_ih, b_hh, W1, b1, W2, b2, W3, b3):
        import jax, jax.numpy as jnp
        import numpy as np
        N_NODES = 10000
        N_EDGES = 10000
        D = 256
        D_OUT = 256
        NUM_REL = 2
        n_nodes = feat.shape[0]
        S = feat[src]

        def edge_nn(x, W, b):
            h = jax.nn.relu(x @ W.T + b)
            return jax.nn.relu(h @ W.T + b)
        msgs = jnp.zeros_like(S)
        for r in range(W_rel.shape[0]):
            msgs = jnp.where((rel == r)[:, None], edge_nn(S, W_rel[r], b_rel[r]), msgs)
        agg = jax.ops.segment_sum(msgs, dst, num_segments=n_nodes)
        gates = agg @ W_ih.T + b_ih + b_hh
        i, f, g, o = jnp.split(gates, 4, axis=-1)
        c = jax.nn.sigmoid(i) * jnp.tanh(g)
        hn = jax.nn.sigmoid(o) * jnp.tanh(c)
        x = jax.nn.relu(hn @ W1.T + b1)
        x = jax.nn.relu(x @ W2.T + b2)
        return x @ W3.T + b3
    deg = jnp.maximum(jax.ops.segment_sum(jnp.ones(dst.shape, jnp.float32), dst, num_segments=3125), 1.0)
    deg_isqrt = deg ** (-0.5)
    h = jnp.maximum(_layernorm(x, axis=-1), 0.0)
    x = x + _L0_gnn_ref(h, src, dst, edge_weight, deg_isqrt[:, None], L0_gnn_w1, L0_gnn_gamma1, L0_gnn_beta1, L0_gnn_w2, L0_gnn_eps_weight, L0_gnn_gamma_h, L0_gnn_beta_h)
    h = jnp.maximum(_layernorm(x, axis=-1), 0.0)
    x = x + _L1_gnn_ref(h, src, dst, edge_type_2, L1_gnn_W_rel, L1_gnn_b_rel, L1_gnn_W_ih, L1_gnn_b_ih, L1_gnn_b_hh, L1_gnn_W1, L1_gnn_b1, L1_gnn_W2, L1_gnn_b2, L1_gnn_W3, L1_gnn_b3)
    return x

_drawn_inputs = setup_inputs


def setup_inputs(seed=0):
    import zlib

    import numpy as np

    out = dict(_drawn_inputs(seed))
    spreads = {'L0_gnn_gamma1': (1.0, 0.2),
     'L0_gnn_beta1': (0.0, 0.1),
     'L0_gnn_gamma_h': (1.0, 0.2),
     'L0_gnn_beta_h': (0.0, 0.1)}
    factors = {'L1_gnn_b_rel': 3.849, 'L1_gnn_b_ih': 32.6, 'L1_gnn_b_hh': 30.952, 'L1_gnn_b1': 3.483}
    for name, (base, spread) in spreads.items():
        noise = np.random.default_rng([zlib.crc32(name.encode()), seed]).standard_normal(out[name].shape)
        drawn = base * np.exp(spread * noise) if base else spread * noise
        out[name] = jnp.asarray(drawn.astype(out[name].dtype))
    for name, factor in factors.items():
        out[name] = (out[name] * factor).astype(out[name].dtype)
    return out
```

```python
from contextlib import ExitStack

import numpy as np

import concourse.bass as bass
from concourse import mybir

F32 = mybir.dt.float32
BF16 = mybir.dt.bfloat16
I32 = mybir.dt.int32
ALU = mybir.AluOpType
ACT = mybir.ActivationFunctionType
AX_X = mybir.AxisListType.X
ds = bass.ds

P = 128
N = 3125
D = 256
E = 53125
CH = 13
G = 32
GP = G + 2
EG = CH * P
NPAD = G * EG - E
T = 25
TB = 5
NB = T // TB
BN = TB * P
NP = T * P
RUNS = G // 2
BLK = 196
LAST = N - (RUNS - 1) * BLK
HB = BLK // 2
LASTH = LAST - HB
WW = 408
WN = 8
AGW = WW * WN
EPS = 1e-5
assert NPAD >= 0 and RUNS * BLK >= N and AGW >= N + P and T * P >= N
assert GP * CH >= G * CH

COLS = {}
_at = 0
for _name, _n in (
    ("w1", 2 * D), ("w2", 2 * D), ("wrel", 4 * D), ("wih", 2 * 6 * P), ("m1", 2 * P), ("m2", P), ("m3", D),
    ("g1", 2), ("be1", 2), ("gh", 2), ("beh", 2), ("brel", 4), ("bih", 6), ("bhh", 6), ("b1", 1), ("b2", 1),
    ("eps", 1), ("brow", 2 * D), ("b3", D), ("ident", P), ("iota", WW), ("lim", G),
):
    COLS[_name] = (_at, _at + _n)
    _at += _n
NCOLS = _at


class Steps:

    def __init__(self, eng, sem):
        self.eng, self.sem, self.base, self.n = eng, sem, 0, 0

    def mark(self, ins):
        ins.then_inc(self.sem, 1)
        self.n += 1

    def sync(self):
        self.eng.wait_ge(self.sem, self.base + self.n)

    def enter(self, turn, per):
        self.before = self.base + self.n
        self.per = per
        self.base, self.n = turn * per + self.before, 0

    def leave(self, turns):
        assert self.n == self.per, (self.n, self.per)
        self.base, self.n = self.before + turns * self.per, 0


def wait_alone(eng, sem, value):
    eng.wait_ge(sem, value)
    eng.nop(nofuse=True)


def build(nc, x, edges, weights, firsts, params, out):
    tab = nc.dram_tensor("ln_table", (NP, D), F32, kind="Internal").ap()
    mtab = nc.dram_tensor("message_table", (2 * NP, D), F32, kind="Internal").ap()
    x1d = nc.dram_tensor("layer0_out", (NP, D), F32, kind="Internal").ap()

    with ExitStack() as ctx:
        def sb(name, shape, dt=F32):
            return ctx.enter_context(nc.sbuf_tensor(name, shape, dt))

        def sem(name):
            return ctx.enter_context(nc.semaphore(name))

        ps = ctx.enter_context(nc.psum_tensor("ps", [P, 8, 512], F32))
        par = sb("par", [P, NCOLS])
        xh = sb("xh", [P, T, D])
        h0 = sb("h0", [P, T, D])
        h0t = sb("h0t", [P, 2, NP])
        nodes = sb("nodes", [P, 2, AGW])
        deg = sb("deg", [P, AGW])
        msg = sb("msg", [P, 2 * CH, D])
        oh = sb("oh", [P, 2 * CH, P])
        ohb = sb("ohb", [P, 2 * CH, P], BF16)
        ed = sb("ed", [P, GP, 3, CH], I32)
        ew = sb("ew", [P, GP, CH])
        st = sb("st", [P, 2, 3, CH], I32)
        stw = sb("stw", [P, 2, CH])
        bi = sb("bi", [P, GP], I32)
        ones = sb("ones", [P, P], BF16)
        onef = sb("onef", [P, 1])
        yb = sb("yb", [P, 2, BLK])
        lst = sb("lst", [P, TB, 6])
        lm = sb("lm", [P, 2, 6, TB])
        zst = sb("zst", [P, 2, RUNS, 6])
        yst = sb("yst", [P, 2, RUNS, 6])
        bnv = sb("bnv", [P, 2, 2, 2])
        bns = sb("bns", [P, 2, 4, 2])
        bg = sb("bg", [P, 6])
        tmp = sb("tmp", [P, G * CH])
        tmp2 = sb("tmp2", [P, G * CH])
        cnt = sb("cnt", [P, 4])
        badi = sb("badi", [1, 1], I32)
        epsc = sb("epsc", [P, 1])
        woff = sb("woff", [P, 1])
        flat = h0t[:, :, :].rearrange("p h n -> p (h n)")
        r_sb = flat[:, 0:2 * BN].rearrange("p (h n) -> p h n", h=2)
        h1 = flat[:, 2 * BN:4 * BN].rearrange("p (t d) -> p t d", t=TB)
        h1t = sb("h1t", [P, 2, BN])
        hid = h0[:, 0:10, :].rearrange("p t d -> p (t d)").rearrange("p (r h n) -> p r h n", r=2, h=2)
        mst = h0[:, 10:20, :].rearrange("p (t r) d -> p t r d", r=2)
        at = 0

        def view(n, parts=P):
            nonlocal at
            at += n
            return flat[0:parts, at - n:at]

        gat = view(6 * BLK).rearrange("p (k n) -> p k n", k=6)
        cc = view(6 * BLK).rearrange("p (k h n) -> p k h n", k=3, h=2)
        mm1, mm2 = view(BLK), view(BLK)
        at = 8 * BN
        xb = view(2 * D, HB).rearrange("p (a d) -> p a d", a=2)
        ost = view(2 * D, HB).rearrange("p (a d) -> p a d", a=2)

        def col(name):
            return par[:, COLS[name][0]:COLS[name][1]]

        w1 = col("w1").rearrange("p (i o) -> p i o", i=2)
        w2 = col("w2").rearrange("p (i o) -> p i o", i=2)
        wrel = col("wrel").rearrange("p (r i o) -> p r i o", r=2, i=2)
        wih = col("wih").rearrange("p (i k o) -> p i k o", i=2, k=6)
        m1 = col("m1").rearrange("p (i o) -> p i o", i=2)
        m2, m3 = col("m2"), col("m3")
        brel = col("brel").rearrange("p (r h) -> p r h", r=2)
        brow = col("brow").rearrange("p (r d) -> p r d", r=2)
        ident, iota = col("ident"), col("iota")

        s_x = [sem(f"s_xin{b}") for b in range(NB)]
        s_par, s_edge = sem("s_par"), sem("s_edge")
        s_dve, s_act = sem("s_dve"), sem("s_act")
        s_const = sem("s_const")
        s_var, s_std, s_rstd, s_h0, s_tab = (sem(n) for n in ("s_var", "s_std", "s_rstd", "s_h0", "s_tab"))
        s_tr, s_h0t = sem("s_tr"), sem("s_h0t")
        s_st = [sem(f"s_st{h}") for h in range(2)]
        s_oh = [sem(f"s_oh{h}") for h in range(2)]
        s_slot = [sem(f"s_slot{k}") for k in range(2 * CH)]
        s_sum = [sem(f"s_sum{h}") for h in range(2)]
        s_add = [sem(f"s_add{h}") for h in range(2)]
        s_cnt, s_cntp, s_flag = sem("s_cnt"), sem("s_cntp"), sem("s_flag")
        zs, zg = ({n: sem(k + n) for n in ("yb", "mm", "cp", "st", "degm", "degs")} for k in ("z_", "zg_"))
        s_bn = [sem(f"s_bn{k}") for k in range(2)]
        s_bnv = [sem(f"s_bnv{k}") for k in range(2)]
        s_bnd = [sem(f"s_bnd{k}") for k in range(2)]
        s_hr = sem("s_hr")
        s_w2 = [sem(f"s_w2{k}") for k in range(2)]
        s_y = [sem(f"s_y{k}") for k in range(2)]
        s_r, s_ta, s_x1, s_var1, s_std1, s_rstd1, s_h1, s_tb, s_h1t = (
            sem(n) for n in ("s_r", "s_ta", "s_x1", "s_var1", "s_std1", "s_rstd1", "s_h1", "s_tb", "s_h1t"))
        s_l1, s_hid, s_l2, s_l2a, s_m, s_mtab, s_x1d, s_zero = (
            sem(n) for n in ("s_l1", "s_hid", "s_l2", "s_l2a", "s_m", "s_mtab", "s_x1d", "s_zero"))
        ms, mg = ({n: sem(k + n) for n in (
            "gmm", "gact", "c", "tc", "hn", "w1", "a1", "w2", "a2", "w3", "out", "xb", "st0", "st1")}
            for k in ("m_", "mg_"))
        g_slot = [sem(f"g_slot{c}") for c in range(CH)]
        g_st, g_oh, g_sum, g_add, g_zero, g_off = (
            sem(n) for n in ("g_st", "g_oh", "g_sum", "g_add", "g_zero", "g_off"))

        def if_outside(eng):
            eng.wait_ge(s_flag, 1)
            return eng.If(eng.value_load(badi[0:1, 0:1], min_val=0, max_val=1 << 17) > 0)

        def windows(eng, layer, group, window=None):
            with eng.Fori(0, T) as w:
                if window:
                    window(w)
                with eng.Fori(0, G) as g:
                    group(w, g, w * G + g + layer * T * G)

        block = ctx.enter_context(nc.Block())

        @block.sync
        def _(sp):
            for b in range(NB):
                sp.dma_start(xh[:, b * TB:(b + 1) * TB, :],
                             x[b * BN:(b + 1) * BN, :].rearrange("(t p) d -> p t d", p=P)).then_inc(s_x[b], 16)
            for b in range(NB):
                sp.wait_ge(s_h0, b + 1)
                sp.dma_start(tab[b * BN:(b + 1) * BN, :].rearrange("(t p) d -> p t d", p=P),
                             h0[:, b * TB:(b + 1) * TB, :]).then_inc(s_tab, 16)
            with sp.Fori(0, NB) as b:
                sp.wait_ge(s_x1, b + 1)
                sp.dma_start(x1d[ds(b * BN, BN), :].rearrange("(t p) d -> p t d", p=P),
                             xh[:, ds(b * TB, TB), :]).then_inc(s_x1d, 16)
                sp.wait_ge(s_m, (b + 1) * TB)
                for r in range(2):
                    sp.dma_start(mtab[ds(b * BN + r * NP, BN), :].rearrange("(t p) d -> p t d", p=P),
                                 mst[:, :, r, :]).then_inc(s_mtab, 16)

            def load_rows(S, n):
                sp.wait_ge(S["out"], n)
                sp.dma_start(xb[:, :, :], x1d[ds(n * BLK, BLK), :].rearrange("(a p) d -> p a d", p=HB)
                             ).then_inc(S["xb"], 16)

            def blocks(S):
                with sp.Fori(0, RUNS - 1) as n:
                    load_rows(S, n)
                    sp.wait_ge(S["out"], n + 1)
                    sp.dma_start(out[ds(n * BLK, BLK), :].rearrange("(a p) d -> p a d", p=HB),
                                 ost[:, :, :]).then_inc(S["st0"], 16)
                load_rows(S, RUNS - 1)
                sp.wait_ge(S["out"], RUNS)
                at = (RUNS - 1) * BLK
                sp.dma_start(out[at:at + HB, :], ost[:, 0, :]).then_inc(S["st1"], 16)
                sp.dma_start(out[at + HB:N, :], ost[0:LASTH, 1, :]).then_inc(S["st1"], 16)
                sp.wait_ge(S["st0"], 16 * (RUNS - 1))
                sp.wait_ge(S["st1"], 32)

            sp.wait_ge(s_x1d, 16 * NB)
            blocks(ms)
            with if_outside(sp):
                blocks(mg)

        @block.gpsimd
        def _(pool):
            pool.memset(ones[:, :], 1.0)
            pool.memset(onef[:, :], 1.0)
            pool.memset(epsc[:, :], EPS)
            pool.memset(nodes[:, :, :], 0.0)
            pool.memset(deg[:, :], 0.0).then_inc(s_const, 1)

            def gathers(h, turn, table, row, written):
                pool.wait_ge(*written)
                wait_alone(pool, s_st[h], turn + 1)
                for c in range(CH):
                    pool.indirect_dma_start(
                        msg[:, h * CH + c, :], None, table,
                        bass.IndirectOffsetOnAxis(ap=st[:, h, row, c:c + 1], axis=0)
                    ).then_inc(s_slot[h * CH + c], 16)

            def gather_all(layer, table, row):
                def group(w, g, t):
                    wait_alone(pool, g_st, t + 1)
                    for c in range(CH):
                        pool.indirect_dma_start(
                            msg[:, c, :], None, table,
                            bass.IndirectOffsetOnAxis(ap=st[:, 0, row, c:c + 1], axis=0)).then_inc(g_slot[c], 16)
                windows(pool, layer, group)

            with pool.Fori(0, RUNS) as i:
                for h in range(2):
                    gathers(h, i, tab, 0, (s_tab, 16 * NB))
            with if_outside(pool):
                gather_all(0, tab, 0)
            with pool.Fori(0, RUNS) as i:
                for h in range(2):
                    gathers(h, i + RUNS + (1 - h), mtab, 1, (s_mtab, 32 * NB))
            with if_outside(pool):
                gather_all(1, mtab, 1)

        @block.tensor
        def _(pe):
            pe.wait_ge(s_par, 16)
            for t in range(T):
                if t % TB == 0:
                    pe.wait_ge(s_h0, t // TB + 1)
                if t >= 2:
                    pe.wait_ge(s_h0t, t - 1)
                for h in range(2):
                    last = pe.transpose(ps[:, 3 + t % 2, h * P:(h + 1) * P], h0[:, t, h * P:(h + 1) * P], ident)
                last.then_inc(s_tr, 1)
            pe.wait_ge(s_const, 1)

            def products(h, turn, layer, chunks):
                if chunks[0] == 0:
                    pe.wait_ge(s_oh[h], turn + (1 - h) * layer + 1)
                    pe.wait_ge(s_add[h], turn)
                last = chunk_products(h, layer, chunks, s_slot, turn * 16 + 16)
                if chunks[-1] == CH - 1:
                    last.then_inc(s_sum[h], 1)

            def chunk_products(h, layer, chunks, slots, landed):
                for c in chunks:
                    k = h * CH + c
                    pe.wait_ge(slots[k], landed)
                    pe.matmul(ps[:, h, 0:P], msg[:, k, 0:P], oh[:, k, :], start=(c == 0), stop=(c == CH - 1),
                              skip_group_check=True)
                    last = pe.matmul(ps[:, h, P:2 * P], msg[:, k, P:2 * P], oh[:, k, :], start=False,
                                     stop=(c == CH - 1), skip_group_check=True)
                    if layer == 0:
                        last = pe.matmul(ps[:, h, 2 * P:3 * P], ones[:, :], ohb[:, k, :], start=False,
                                         stop=(c == CH - 1), skip_group_check=True)
                return last

            def sum_all(layer):
                def group(w, g, t):
                    pe.wait_ge(g_oh, t + 1)
                    pe.wait_ge(g_add, t)
                    chunk_products(0, layer, range(CH), g_slot, t * 16 + 16).then_inc(g_sum, 1)
                windows(pe, layer, group)

            def z_mm(S, n, w):
                pe.wait_ge(S["yb"], n + 1)
                pe.wait_ge(S["cp"], n)
                for o in range(2):
                    for i in range(2):
                        last = pe.matmul(ps[:, 2, o * BLK:o * BLK + w], w1[:, i, o * P:(o + 1) * P], yb[:, i, 0:w],
                                         start=(i == 0), stop=(i == 1), skip_group_check=True)
                last.then_inc(S["mm"], 1)

            early, late = list(range(6)), list(range(6, CH))

            def edge_loop(layer, dense):
                o = layer * RUNS
                full = early + late
                products(0, o, layer, full)
                products(1, o, layer, full)
                products(0, 1 + o, layer, full)
                with pe.Fori(1, RUNS - 1) as i:
                    dense(i - 1, BLK, lambda part: products(1, i + o, layer, part), i + o + 1, None)
                    products(0, i + o + 1, layer, full)
                dense(RUNS - 2, BLK, lambda part: products(1, RUNS - 1 + o, layer, part), RUNS + o, None)
                dense(RUNS - 1, LAST, None, RUNS + o, RUNS + o)

            def dense0(n, w, more, added_a, added_b):
                if more:
                    more(early)
                z_mm(zs, n, w)
                if more:
                    more(late)

            def count_outside():
                pe.wait_ge(s_cnt, 1)
                pe.matmul(ps[0:1, 5, 0:1], cnt[:, 2:3], onef[:, :], start=True, stop=True).then_inc(s_cntp, 1)

            count_outside()
            edge_loop(0, dense0)
            with if_outside(pe):
                sum_all(0)
                with pe.Fori(0, RUNS - 1) as n:
                    z_mm(zg, n, BLK)
                z_mm(zg, RUNS - 1, LAST)

            def w2_mm(n, turn, k, w):
                pe.wait_ge(s_hr, n + 1)
                pe.wait_ge(s_y[k], turn)
                for o in range(2):
                    for i in range(2):
                        last = pe.matmul(ps[:, 6 + k, o * BLK:o * BLK + w], w2[:, i, o * P:(o + 1) * P],
                                         nodes[:, i, ds(n * BLK, w)], start=(i == 0), stop=(i == 1),
                                         skip_group_check=True)
                last.then_inc(s_w2[k], 1)

            with pe.Fori(0, RUNS // 2 - 1) as j:
                for k in range(2):
                    w2_mm(j * 2 + k, j, k, BLK)
            w2_mm(RUNS - 2, RUNS // 2 - 1, 0, BLK)
            w2_mm(RUNS - 1, RUNS // 2 - 1, 1, LAST)

            def to_nodes(b):
                pe.wait_ge(s_r, b + 1)
                pe.wait_ge(s_h1t, b)
                for t in range(TB):
                    for h in range(2):
                        last = pe.transpose(ps[:, 3 + t // 2, (t % 2) * D + h * P:(t % 2) * D + (h + 1) * P],
                                            r_sb[:, h, t * P:(t + 1) * P], ident)
                last.then_inc(s_ta, 1)

            def to_features(b):
                pe.wait_ge(s_h1, b + 1)
                pe.wait_ge(s_x1, b + 1)
                for t in range(TB):
                    for h in range(2):
                        last = pe.transpose(ps[:, 3 + t // 2, (t % 2) * D + h * P:(t % 2) * D + (h + 1) * P],
                                            h1[:, t, h * P:(h + 1) * P], ident)
                last.then_inc(s_tb, 1)

            def first_mm(b):
                pe.wait_ge(s_h1t, b + 1)
                k = 0
                for r in range(2):
                    for o in range(2):
                        for c in range(2):
                            pe.wait_ge(s_hid, b * 8 + (k - 1 if k >= 2 else 0))
                            for i in range(2):
                                last = pe.matmul(ps[:, 6 + k % 2, 0:BN // 2], wrel[:, r, i, o * P:(o + 1) * P],
                                                 h1t[:, i, c * (BN // 2):(c + 1) * (BN // 2)],
                                                 start=(i == 0), stop=(i == 1))
                            last.then_inc(s_l1, 1)
                            k += 1

            def second_mm(b, tiles):
                pe.wait_ge(s_hid, b * 8 + 8)
                for t in tiles:
                    pe.wait_ge(s_l2a, b * TB + (t - 1 if t >= 2 else 0))
                    for r in range(2):
                        for i in range(2):
                            last = pe.matmul(ps[:, t % 2, r * D:(r + 1) * D], hid[:, r, i, t * P:(t + 1) * P],
                                             wrel[:, r, i, :], start=(i == 0), stop=(i == 1), skip_group_check=True)
                    last.then_inc(s_l2, 1)

            to_nodes(0)
            to_features(0)
            with pe.Fori(0, NB - 1) as b:
                to_nodes(b + 1)
                first_mm(b)
                second_mm(b, [0, 1])
                to_features(b + 1)
                second_mm(b, [2, 3, 4])
            first_mm(NB - 1)
            second_mm(NB - 1, list(range(TB)))

            def dense1(n, w, more, added_a, added_b, S=ms):
                if more:
                    more([0])
                if added_a is not None:
                    pe.wait_ge(s_add[0], added_a)
                if added_b is not None:
                    pe.wait_ge(s_add[1], added_b)
                pe.wait_ge(S["gact"], n)
                for k in range(6):
                    for i in range(2):
                        last = pe.matmul(ps[:, 3 + k // 2, (k % 2) * BLK:(k % 2) * BLK + w], wih[:, i, k, :],
                                         nodes[:, i, ds(n * BLK, w)], start=(i == 0), stop=(i == 1),
                                         skip_group_check=True)
                last.then_inc(S["gmm"], 1)
                if more:
                    more([1, 2, 3, 4, 5])
                pe.wait_ge(S["hn"], n + 1)
                for i in range(2):
                    last = pe.matmul(ps[:, 2, 0:w], m1[:, i, :], cc[:, 2, i, 0:w], start=(i == 0), stop=(i == 1),
                                     skip_group_check=True)
                last.then_inc(S["w1"], 1)
                if more:
                    more([6, 7, 8])
                pe.wait_ge(S["a1"], n + 1)
                pe.matmul(ps[:, 2, BLK:BLK + w], m2, mm1[:, 0:w], start=True, stop=True,
                          skip_group_check=True).then_inc(S["w2"], 1)
                if more:
                    more([9, 10, 11, 12])
                pe.wait_ge(S["a2"], n + 1)
                pe.wait_ge(S["out"], n)
                pe.matmul(ps[0:HB, 6, 0:D], mm2[:, 0:HB], m3, start=True, stop=True, skip_group_check=True)
                pe.matmul(ps[0:w - HB, 6, D:2 * D], mm2[:, HB:w], m3, start=True, stop=True,
                          skip_group_check=True).then_inc(S["w3"], 1)

            edge_loop(1, dense1)
            with if_outside(pe):
                sum_all(1)
                pe.wait_ge(g_add, 2 * T * G)
                with pe.Fori(0, RUNS - 1) as n:
                    dense1(n, BLK, None, None, None, mg)
                dense1(RUNS - 1, LAST, None, None, None, mg)

        @block.scalar
        def _(act):
            act.dma_start(ed[:, :, :, :], edges).then_inc(s_edge, 16)
            act.dma_start(bi[:, :], firsts).then_inc(s_edge, 16)
            act.dma_start(ew[:, :, :], weights).then_inc(s_edge, 16)
            act.dma_start(par[:, :], params).then_inc(s_par, 16)
            act.wait_ge(s_const, 1)

            def spread(b, k, var, done, count):
                act.wait_ge(var, count)
                act.activation(lm[:, k, 3, :], lm[:, k, 2, :], ACT.Sqrt, bias=epsc[:, 0:1]).then_inc(done, 1)

            def normal0(b):
                act.wait_ge(s_rstd, b + 1)
                for t in range(TB):
                    last = act.activation(h0[:, b * TB + t, :], xh[:, b * TB + t, :], ACT.Relu,
                                          bias=lm[:, b % 2, 5, t:t + 1], scale=lm[:, b % 2, 4, t:t + 1])
                last.then_inc(s_h0, 1)

            spread(0, 0, s_var, s_std, 1)
            for b in range(NB):
                if b + 1 < NB:
                    spread(b + 1, (b + 1) % 2, s_var, s_std, b + 2)
                normal0(b)
            act.wait_ge(s_par, 16)
            for t in range(T):
                act.wait_ge(s_tr, t + 1)
                act.activation(h0t[:, :, t * P:(t + 1) * P],
                               ps[:, 3 + t % 2, 0:2 * P].rearrange("p (h n) -> p h n", h=2), ACT.Copy,
                               scale=col("eps")[:, 0:1]).then_inc(s_h0t, 1)

            def z_act(S, n, w):
                act.wait_ge(S["degm"], n + 1)
                act.activation(deg[:, ds(n * BLK, w)], deg[:, ds(n * BLK, w)], ACT.Sqrt).then_inc(S["degs"], 1)
                act.wait_ge(S["mm"], n + 1)
                act.activation(nodes[:, :, ds(n * BLK, w)],
                               ps[:, 2, 0:2 * BLK].rearrange("p (h n) -> p h n", h=2)[:, :, 0:w],
                               ACT.Copy).then_inc(S["cp"], 1)

            def z_all(S):
                with act.Fori(0, RUNS - 1) as n:
                    z_act(S, n, BLK)
                z_act(S, RUNS - 1, LAST)

            z_all(zs)
            with if_outside(act):
                z_all(zg)

            def bn_std(k):
                act.wait_ge(s_bnv[k], 1)
                act.activation(bns[:, k, 0, :], bnv[:, k, :, 1], ACT.Sqrt, bias=epsc[:, 0:1]).then_inc(s_bnd[k], 1)

            bn_std(0)
            act.wait_ge(s_bn[0], 1)

            def relu_z(n, w):
                for h in range(2):
                    last = act.activation(nodes[:, h, ds(n * BLK, w)], nodes[:, h, ds(n * BLK, w)], ACT.Relu,
                                          bias=bns[:, 0, 3, h:h + 1], scale=bns[:, 0, 2, h:h + 1])
                last.then_inc(s_hr, 1)

            with act.Fori(0, RUNS - 1) as n:
                relu_z(n, BLK)
            relu_z(RUNS - 1, LAST)
            bn_std(1)
            act.wait_ge(s_bn[1], 1)

            def relu_y(b):
                act.wait_ge(s_ta, b)
                for h in range(2):
                    last = act.activation(r_sb[:, h, :], nodes[:, h, ds(b * BN, BN)], ACT.Relu,
                                          bias=bns[:, 1, 3, h:h + 1], scale=bns[:, 1, 2, h:h + 1])
                last.then_inc(s_r, 1)

            def normal1(b, tiles):
                if tiles[0] == 0:
                    act.wait_ge(s_rstd1, b + 1)
                    act.wait_ge(s_tb, b)
                for t in tiles:
                    last = act.activation(h1[:, t, :], xh[:, ds(b * TB + t, 1), :].rearrange("p a d -> p (a d)"),
                                          ACT.Relu, bias=lm[:, 0, 5, t:t + 1], scale=lm[:, 0, 4, t:t + 1])
                if tiles[-1] == TB - 1:
                    last.then_inc(s_h1, 1)

            def hidden(b, ks):
                for k in ks:
                    r, o, c = k // 4, k // 2 % 2, k % 2
                    act.wait_ge(s_l1, b * 8 + k + 1)
                    act.activation(hid[:, r, o, c * (BN // 2):(c + 1) * (BN // 2)], ps[:, 6 + k % 2, 0:BN // 2],
                                   ACT.Relu, bias=brel[:, r, o:o + 1]).then_inc(s_hid, 1)

            def message_relu(b):
                for t in range(TB):
                    act.wait_ge(s_l2a, b * TB + t + 1)
                    act.activation(mst[:, t, :, :], mst[:, t, :, :], ACT.Relu).then_inc(s_m, 1)

            relu_y(0)
            spread(0, 0, s_var1, s_std1, 1)
            normal1(0, list(range(TB)))
            with act.Fori(0, NB - 1) as b:
                relu_y(b + 1)
                hidden(b, [0, 1, 2, 3, 4, 5])
                spread(b + 1, 0, s_var1, s_std1, b + 2)
                hidden(b, [6])
                normal1(b + 1, [0, 1, 2])
                hidden(b, [7])
                normal1(b + 1, [3, 4])
                message_relu(b)
            hidden(NB - 1, list(range(8)))
            message_relu(NB - 1)

            def mlp_act(S, n, w):
                act.wait_ge(S["gmm"], n + 1)
                for k in range(6):
                    last = act.activation(gat[:, k, 0:w], ps[:, 3 + k // 2, (k % 2) * BLK:(k % 2) * BLK + w],
                                          ACT.Tanh if k in (2, 3) else ACT.Sigmoid, bias=bg[:, k:k + 1])
                last.then_inc(S["gact"], 1)
                act.wait_ge(S["c"], n + 1)
                act.activation(cc[:, 1, :, 0:w], cc[:, 0, :, 0:w], ACT.Tanh).then_inc(S["tc"], 1)
                act.wait_ge(S["w1"], n + 1)
                act.activation(mm1[:, 0:w], ps[:, 2, 0:w], ACT.Relu, bias=col("b1")).then_inc(S["a1"], 1)
                act.wait_ge(S["w2"], n + 1)
                act.activation(mm2[:, 0:w], ps[:, 2, BLK:BLK + w], ACT.Relu, bias=col("b2")).then_inc(S["a2"], 1)

            def mlp_all(S):
                with act.Fori(0, RUNS - 1) as n:
                    mlp_act(S, n, BLK)
                mlp_act(S, RUNS - 1, LAST)

            mlp_all(ms)
            with if_outside(act):
                mlp_all(mg)

        @block.vector
        def _(dve):
            own = Steps(dve, s_dve)
            dve.wait_ge(s_edge, 48)
            dve.scalar_tensor_tensor(out=ed[:, :, 1, :], in0=ed[:, :, 1, :], scalar=float(NP), in1=ed[:, :, 0, :],
                                     op0=ALU.mult, op1=ALU.add)
            own.mark(dve.tensor_tensor(ed[:, :, 2, :].bitcast(F32), ed[:, :, 2, :],
                                       bi[:, :].rearrange("p (g o) -> p g o", o=1).broadcast_to([P, GP, CH]),
                                       ALU.subtract))
            dve.wait_ge(s_const, 1)

            def row_moments(k, var):
                me, mo, ve, vo = lst[:, :, 1], lst[:, :, 4], lst[:, :, 2], lst[:, :, 5]
                own.sync()
                dve.tensor_tensor(lm[:, k, 0, :], me, mo, ALU.add)
                dve.tensor_tensor(lm[:, k, 1, :], me, mo, ALU.subtract)
                own.mark(dve.tensor_tensor(lm[:, k, 2, :], ve, vo, ALU.add))
                own.sync()
                dve.tensor_scalar(lm[:, k, 0, :], lm[:, k, 0, :], 0.5, None, ALU.mult)
                own.mark(dve.scalar_tensor_tensor(out=lm[:, k, 1, :], in0=lm[:, k, 1, :], scalar=D / 4.0,
                                                  in1=lm[:, k, 1, :], op0=ALU.mult, op1=ALU.mult))
                own.sync()
                own.mark(dve.tensor_tensor(lm[:, k, 2, :], lm[:, k, 2, :], lm[:, k, 1, :], ALU.add))
                own.sync()
                dve.tensor_scalar(lm[:, k, 2, :], lm[:, k, 2, :], 1.0 / D, None, ALU.mult).then_inc(var, 1)

            def row_scales(k, std, count, done):
                dve.wait_ge(std, count)
                own.mark(dve.reciprocal(lm[:, k, 4, :], lm[:, k, 3, :]))
                own.sync()
                dve.scalar_tensor_tensor(out=lm[:, k, 5, :], in0=lm[:, k, 0, :], scalar=-1.0, in1=lm[:, k, 4, :],
                                         op0=ALU.mult, op1=ALU.mult).then_inc(done, 1)

            for b in range(NB):
                dve.wait_ge(s_x[b], 16)
                if b >= 2:
                    dve.wait_ge(s_h0, b - 1)
                for t in range(TB):
                    last = dve.bn_stats(lst[:, t, :], xh[:, b * TB + t, :])
                own.mark(last)
                row_moments(b % 2, s_var)
                if b >= 1:
                    row_scales((b - 1) % 2, s_std, b, s_rstd)
            row_scales((NB - 1) % 2, s_std, NB, s_rstd)

            def stage(h, turn, g, layer):
                if layer == 0:
                    dve.tensor_copy(stw[:, h, :], ew[:, ds(g, 1), :].rearrange("p a c -> p (a c)"))
                dve.tensor_copy(st[:, h, :, :], ed[:, ds(g, 1), :, :].rearrange("p a k c -> p (a k) c")
                                ).then_inc(s_st[h], 1)
                dve.wait_ge(s_st[h], turn + (1 - h) * layer + 1)
                one_hots(h, layer).then_inc(s_oh[h], 1)

            def one_hots(h, layer):
                rel = st[:, h, 2, :].bitcast(F32)
                for c in range(CH):
                    k = h * CH + c
                    if layer == 0:
                        dve.tensor_scalar(oh[:, k, :], iota[:, 0:P], rel[:, c:c + 1], stw[:, h, c:c + 1],
                                          ALU.is_equal, ALU.mult)
                        last = dve.tensor_scalar(ohb[:, k, :], iota[:, 0:P], rel[:, c:c + 1], None, ALU.is_equal)
                    else:
                        last = dve.tensor_scalar(oh[:, k, :], iota[:, 0:P], rel[:, c:c + 1], None, ALU.is_equal)
                return last

            def add(h, turn, g, layer):
                dve.wait_ge(s_sum[h], turn + 1)
                base = dve.value_load(bi[0:1, ds(g, 1)], min_val=0, max_val=N - 1)
                dve.wait_ge(s_add[1 - h], turn + h)
                if layer == 0:
                    dve.tensor_tensor(deg[:, ds(base, P)], deg[:, ds(base, P)], ps[:, h, 2 * P:3 * P], ALU.add)
                win = nodes[:, :, ds(base, P)]
                dve.tensor_tensor(win, win, ps[:, h, 0:2 * P].rearrange("p (h n) -> p h n", h=2), ALU.add
                                  ).then_inc(s_add[h], 1)

            def z_in(n, w, S=zs):
                dve.wait_ge(S["mm"], n)
                if S is zg:
                    dve.wait_ge(g_add, T * G)
                elif w == BLK:
                    dve.wait_ge(s_add[0], n + 2)
                else:
                    dve.wait_ge(s_add[1], RUNS)
                dve.tensor_tensor(yb[:, :, 0:w], nodes[:, :, ds(n * BLK, w)], h0t[:, :, ds(n * BLK, w)],
                                  ALU.add).then_inc(S["yb"], 1)
                d = deg[:, ds(n * BLK, w)]
                dve.tensor_scalar(d, d, 1.0, None, ALU.max).then_inc(S["degm"], 1)

            def z_out(n, w, S=zs):
                wait_alone(dve, S["degs"], n + 1)
                d = deg[:, ds(n * BLK, w)]
                dve.reciprocal(d, d)
                wait_alone(dve, S["cp"], n + 1)
                for h in range(2):
                    last = dve.bn_stats(zst[:, h, ds(n, 1), :].rearrange("p a s -> p (a s)"),
                                        nodes[:, h, ds(n * BLK, w)])
                last.then_inc(S["st"], 1)

            def edge_loop(layer, before, after, per):
                o = layer * RUNS
                stage(0, o, 0, layer)
                stage(1, o, 1, layer)
                if layer == 0:
                    outside()
                add(0, o, 0, layer)
                stage(0, 1 + o, 2, layer)
                add(1, o, 1, layer)
                stage(1, 1 + o, 3, layer)
                add(0, 1 + o, 2, layer)
                stage(0, 2 + o, 4, layer)
                with dve.Fori(1, RUNS - 1) as i:
                    own.enter(i - 1, per)
                    before(i - 1, BLK)
                    add(1, i + o, i * 2 + 1, layer)
                    stage(1, i + o + 1, i * 2 + 3, layer)
                    after(i - 1, BLK)
                    add(0, i + o + 1, i * 2 + 2, layer)
                    stage(0, i + o + 2, i * 2 + 4, layer)
                    own.leave(RUNS - 2)
                before(RUNS - 2, BLK)
                add(1, RUNS - 1 + o, G - 1, layer)
                after(RUNS - 2, BLK)
                before(RUNS - 1, LAST)
                after(RUNS - 1, LAST)

            def general(layer, before, after, S):
                done = layer * T * G
                if layer == 0:
                    dve.memset(deg[:, :], 0.0)
                dve.memset(nodes[:, :, :], 0.0).then_inc(g_zero, 1)
                dve.memset(woff[:, :], -float(P)).then_inc(g_off, 1)
                dve.wait_ge(g_zero, layer + 1)

                def window(w):
                    dve.wait_ge(g_off, w + layer * (T + 1) + 1)
                    dve.tensor_scalar(woff[:, :], woff[:, :], float(P), None, ALU.add).then_inc(g_off, 1)
                    wait_alone(dve, g_off, w + layer * (T + 1) + 2)

                def group(w, g, t):
                    dve.tensor_copy(stw[:, 0, :], ew[:, ds(g, 1), :].rearrange("p a c -> p (a c)"))
                    dve.scalar_tensor_tensor(
                        out=st[:, 0, 2, :].bitcast(F32),
                        in0=ed[:, ds(g, 1), 2, :].rearrange("p a c -> p (a c)").bitcast(F32), scalar=woff[:, 0:1],
                        in1=bi[:, ds(g, 1)].broadcast_to([P, CH]), op0=ALU.subtract, op1=ALU.add)
                    dve.tensor_copy(st[:, 0, 0:2, :], ed[:, ds(g, 1), 0:2, :].rearrange("p a k c -> p (a k) c")
                                    ).then_inc(g_st, 1)
                    dve.wait_ge(g_st, t + 1)
                    one_hots(0, layer).then_inc(g_oh, 1)
                    dve.wait_ge(g_sum, t + 1)
                    if layer == 0:
                        d = deg[:, ds(w * P, P)]
                        dve.tensor_tensor(d, d, ps[:, 0, 2 * P:3 * P], ALU.add)
                    win = nodes[:, :, ds(w * P, P)]
                    dve.tensor_tensor(win, win, ps[:, 0, 0:2 * P].rearrange("p (h n) -> p h n", h=2), ALU.add
                                      ).then_inc(g_add, 1)
                    wait_alone(dve, g_add, t + 1)

                windows(dve, layer, group, window)
                with dve.Fori(0, RUNS - 1) as n:
                    own.enter(n, layer)
                    before(n, BLK, S)
                    after(n, BLK, S)
                    own.leave(RUNS - 1)
                before(RUNS - 1, LAST, S)
                after(RUNS - 1, LAST, S)

            def outside():
                rel = ed[:, 0:G, 2, :].bitcast(F32)
                t1 = tmp[:, :].rearrange("p (g c) -> p g c", g=G)
                t2 = tmp2[:, :].rearrange("p (g c) -> p g c", g=G)
                own.mark(dve.tensor_scalar(t1, rel, 0.0, None, ALU.is_lt))
                own.sync()
                own.mark(dve.scalar_tensor_tensor(out=t2, in0=rel, scalar=float(P - 1), in1=t1, op0=ALU.is_gt,
                                                  op1=ALU.add))
                own.sync()
                dve.reduce_sum(cnt[:, 0:1], tmp2[:, :], axis=AX_X)
                own.mark(dve.tensor_tensor(tmp[:, 0:G], bi[:, 0:G], col("lim"), ALU.is_lt))
                own.sync()
                own.mark(dve.reduce_sum(cnt[:, 1:2], tmp[:, 0:G], axis=AX_X))
                own.sync()
                dve.tensor_tensor(cnt[:, 2:3], cnt[:, 0:1], cnt[:, 1:2], ALU.add).then_inc(s_cnt, 1)
                dve.wait_ge(s_cntp, 1)
                dve.tensor_scalar(badi[:, :], ps[0:1, 5, 0:1], -float(NPAD), None, ALU.add).then_inc(s_flag, 1)
                for b in range(NB):
                    sl = slice(b * TB, (b + 1) * TB)
                    last = dve.tensor_tensor(xh[:, sl, :], xh[:, sl, :], h0[:, sl, :], ALU.add)
                own.mark(last)
                own.mark(dve.tensor_tensor(bg[:, :], col("bih"), col("bhh"), ALU.add))

            dve.wait_ge(s_par, 16)
            edge_loop(0, z_in, z_out, 0)
            with if_outside(dve):
                general(0, z_in, z_out, zg)
                dve.wait_ge(zg["st"], RUNS)
            dve.wait_ge(zs["st"], RUNS)

            def bn_scales(k, stats, gamma, beta):
                own.sync()
                for h in range(2):
                    last = dve.bn_aggr(bnv[:, k, h, :], stats[:, h, :, :].rearrange("p r s -> p (r s)"))
                last.then_inc(s_bnv[k], 1)
                dve.wait_ge(s_bnd[k], 1)
                own.mark(dve.reciprocal(bns[:, k, 1, :], bns[:, k, 0, :]))
                own.sync()
                own.mark(dve.tensor_tensor(bns[:, k, 2, :], bns[:, k, 1, :], gamma, ALU.mult))
                own.sync()
                own.mark(dve.tensor_tensor(bns[:, k, 1, :], bnv[:, k, :, 0], bns[:, k, 2, :], ALU.mult))
                own.sync()
                dve.tensor_tensor(bns[:, k, 3, :], beta, bns[:, k, 1, :], ALU.subtract).then_inc(s_bn[k], 1)

            bn_scales(0, zst, col("g1"), col("be1"))

            def y_out(n, turn, k, w):
                dve.wait_ge(s_w2[k], turn + 1)
                y = nodes[:, :, ds(n * BLK, w)]
                d = deg[:, ds(n * BLK, w)]
                last = None
                for h in range(2):
                    last = dve.tensor_tensor(nodes[:, h, ds(n * BLK, w)], ps[:, 6 + k, h * BLK:h * BLK + w], d,
                                             ALU.mult)
                last.then_inc(s_y[k], 1)
                wait_alone(dve, s_y[k], turn + 1)
                for h in range(2):
                    last = dve.bn_stats(yst[:, h, ds(n, 1), :].rearrange("p a s -> p (a s)"),
                                        nodes[:, h, ds(n * BLK, w)])
                own.mark(last)

            with dve.Fori(0, RUNS // 2 - 1) as j:
                own.enter(j, 2)
                for k in range(2):
                    y_out(j * 2 + k, j, k, BLK)
                own.leave(RUNS // 2 - 1)
            y_out(RUNS - 2, RUNS // 2 - 1, 0, BLK)
            y_out(RUNS - 1, RUNS // 2 - 1, 1, LAST)
            bn_scales(1, yst, col("gh"), col("beh"))

            banks = ((0, 2, 3), (2, 2, 4), (4, 1, 5))

            def residual(b):
                dve.wait_ge(s_ta, b + 1)
                for t, k, bank in banks:
                    rows = xh[:, ds(b * TB + t, k), :]
                    last = dve.tensor_tensor(rows, rows, ps[:, bank, 0:k * D].rearrange("p (t d) -> p t d", t=k),
                                             ALU.add)
                last.then_inc(s_x1, 1)
                dve.wait_ge(s_x1, b + 1)
                wait_alone(dve, s_h1, b)
                for t in range(TB):
                    last = dve.bn_stats(lst[:, t, :], xh[:, ds(b * TB + t, 1), :].rearrange("p a d -> p (a d)"))
                own.mark(last)
                row_moments(0, s_var1)
                row_scales(0, s_std1, b + 1, s_rstd1)

            def features(b):
                dve.wait_ge(s_tb, b + 1)
                for t, k, bank in banks:
                    last = dve.tensor_copy(
                        h1t[:, :, t * P:(t + k) * P].rearrange("p h (t n) -> p t h n", t=k),
                        ps[:, bank, 0:k * D].rearrange("p (t h n) -> p t h n", t=k, h=2))
                last.then_inc(s_h1t, 1)

            def message_bias(b, tiles):
                if tiles[0] == 0:
                    dve.wait_ge(s_mtab, b * 32)
                for t in tiles:
                    dve.wait_ge(s_l2, b * TB + t + 1)
                    dve.tensor_tensor(mst[:, t, :, :], ps[:, t % 2, :].rearrange("p (r d) -> p r d", r=2), brow,
                                      ALU.add).then_inc(s_l2a, 1)

            residual(0)
            features(0)
            with dve.Fori(0, NB - 1) as b:
                own.enter(b, 5)
                residual(b + 1)
                message_bias(b, [0, 1])
                features(b + 1)
                message_bias(b, [2, 3, 4])
                own.leave(NB - 1)
            dve.wait_ge(s_r, NB)
            own.mark(dve.memset(nodes[:, :, :], 0.0))
            message_bias(NB - 1, list(range(TB)))

            def mlp_in(n, w, S=ms):
                dve.wait_ge(S["gact"], n + 1)
                dve.tensor_tensor(cc[:, 0, :, 0:w], gat[:, 0:2, 0:w], gat[:, 2:4, 0:w], ALU.mult
                                  ).then_inc(S["c"], 1)
                dve.wait_ge(S["tc"], n + 1)
                dve.tensor_tensor(cc[:, 2, :, 0:w], gat[:, 4:6, 0:w], cc[:, 1, :, 0:w], ALU.mult
                                  ).then_inc(S["hn"], 1)

            def mlp_out(n, w, S=ms):
                dve.wait_ge(S["w3"], n + 1)
                dve.wait_ge(S["xb"], n * 16 + 16)
                dve.wait_ge(S["st0"], n * 16)
                b3 = col("b3")
                for a, k in ((0, HB), (1, w - HB)):
                    last = dve.tensor_tensor(ost[0:k, a, :], ps[0:k, 6, a * D:(a + 1) * D], b3[0:k, :], ALU.add)
                own.mark(last)
                own.sync()
                for a, k in ((0, HB), (1, w - HB)):
                    last = dve.tensor_tensor(ost[0:k, a, :], ost[0:k, a, :], xb[0:k, a, :], ALU.add)
                last.then_inc(S["out"], 1)

            edge_loop(1, mlp_in, mlp_out, 1)
            with if_outside(dve):
                general(1, mlp_in, mlp_out, mg)


def kernel(**inputs):
    import concourse.bacc as _bacc
    from concourse.bass_utils import run_bass_kernel_spmd as _run

    g = {k: np.asarray(v) for k, v in inputs.items()}

    def chunks(a, fill):
        full = np.full(GP * EG, fill, a.dtype)
        full[:E] = a
        return full.reshape(GP, CH, P).transpose(2, 0, 1)

    edges = np.stack([chunks(g["src"], 0), chunks(g["edge_type_2"], 0), chunks(g["dst"], -1)], axis=2)
    firsts = np.zeros(GP, np.int32)
    firsts[:G] = g["dst"][::EG]

    def halves(w):
        return np.ascontiguousarray(w.T).reshape(-1, P, w.shape[0]).transpose(1, 0, 2).reshape(P, -1)

    def cols(v):
        return v.reshape(-1, P).T

    used = [0, 1, 4, 5, 6, 7]
    wih = g["L1_gnn_W_ih"].reshape(8, P, D)[used].reshape(6 * P, D)
    pieces = {
        "w1": halves(g["L0_gnn_w1"]), "w2": halves(g["L0_gnn_w2"]),
        "wrel": np.concatenate([halves(g["L1_gnn_W_rel"][r]) for r in range(2)], axis=1),
        "wih": halves(wih), "m1": halves(g["L1_gnn_W1"]), "m2": halves(g["L1_gnn_W2"]), "m3": halves(g["L1_gnn_W3"]),
        "g1": cols(g["L0_gnn_gamma1"]), "be1": cols(g["L0_gnn_beta1"]),
        "gh": cols(g["L0_gnn_gamma_h"]), "beh": cols(g["L0_gnn_beta_h"]), "brel": cols(g["L1_gnn_b_rel"]),
        "bih": cols(g["L1_gnn_b_ih"])[:, used], "bhh": cols(g["L1_gnn_b_hh"])[:, used],
        "b1": cols(g["L1_gnn_b1"]), "b2": cols(g["L1_gnn_b2"]),
        "eps": np.broadcast_to(g["L0_gnn_eps_weight"][None], (P, 1)),
        "brow": np.broadcast_to(g["L1_gnn_b_rel"].reshape(1, -1), (P, 2 * D)),
        "b3": np.broadcast_to(g["L1_gnn_b3"][None], (P, D)),
        "ident": np.eye(P, dtype=np.float32),
        "iota": np.broadcast_to(np.arange(WW, dtype=np.float32), (P, WW)),
        "lim": np.broadcast_to(np.array([max(k - 1, 0) // 2 * BLK for k in range(G)], np.float32), (P, G)),
    }
    params = np.zeros((P, NCOLS), np.float32)
    for name, (a, b) in COLS.items():
        params[:, a:b] = pieces[name]
    x = np.zeros((NP, D), np.float32)
    x[:N] = g["x"]
    arrays = {
        "x": x,
        "edges": np.ascontiguousarray(edges.astype(np.int32)),
        "weights": np.ascontiguousarray(chunks(g["edge_weight"], 0)),
        "firsts": np.ascontiguousarray(np.broadcast_to(firsts, (P, GP))),
        "params": params,
    }
    nc = _bacc.Bacc("TRN2", target_bir_lowering=False, num_devices=1)
    args = [nc.dram_tensor("in_" + n, a.shape, mybir.dt.from_np(a.dtype), kind="ExternalInput").ap()
            for n, a in arrays.items()]
    out = nc.dram_tensor("out", (N, D), F32, kind="ExternalOutput").ap()
    build(nc, *args, out)
    r = _run(nc, [{"in_" + n: a for n, a in arrays.items()}], core_ids=[0])
    return r.results[0]["out"]
```

```python
from contextlib import ExitStack

import numpy as np

import concourse.bass as bass
from concourse import mybir

F32 = mybir.dt.float32
BF16 = mybir.dt.bfloat16
I32 = mybir.dt.int32
ALU = mybir.AluOpType
ACT = mybir.ActivationFunctionType
AX_X = mybir.AxisListType.X
ds = bass.ds

P = 128
N = 3125
D = 256
E = 53125
CH = 13
G = 32
GP = G + 2
EG = CH * P
NPAD = G * EG - E
T = 25
TB = 5
NB = T // TB
BN = TB * P
NP = T * P
STORES = [(b * TB, TB) for b in range(NB - 1)] + [(T - TB, TB - 2), (T - 2, 2)]
LAST_STORES = ((0, 2), (2, 2), (4, 1))
TABLE_STORED = 32 * (NB - 1 + len(LAST_STORES)) + 1
RUNS = G // 2
BLK = 200
LAST = N - (RUNS - 1) * BLK
HB = BLK // 2
LASTH = LAST - HB
AGW = N + P + 11
EPS = 1e-5
assert NPAD >= 0 and RUNS * BLK >= N and AGW >= N + P and T * P >= N
assert GP * CH >= G * CH

EARLY = (("eps", 1), ("ident", P), ("iota", P), ("lim", G), ("bih", 6), ("bhh", 6))
LATE = (
    ("w1", 2 * D), ("w2", 2 * D), ("wrel", 4 * D), ("wih", 2 * 6 * P), ("m1", 2 * P), ("m2", P), ("m3", D),
    ("g1", 2), ("be1", 2), ("gh", 2), ("beh", 2), ("brel", 4), ("b1", 1), ("b2", 1), ("brow", 2 * D), ("b3", D),
)


def columns(names):
    out, at = {}, 0
    for name, n in names:
        out[name] = (at, at + n)
        at += n
    return out, at


EARLY_COLS, NEARLY = columns(EARLY)
LATE_COLS, NLATE = columns(LATE)


class Steps:

    def __init__(self, eng, sem):
        self.eng, self.sem, self.base, self.n = eng, sem, 0, 0

    def mark(self, ins):
        ins.then_inc(self.sem, 1)
        self.n += 1

    def sync(self):
        self.eng.wait_ge(self.sem, self.base + self.n)

    def enter(self, turn, per):
        self.before = self.base + self.n
        self.per = per
        self.base, self.n = turn * per + self.before, 0

    def leave(self, turns):
        assert self.n == self.per, (self.n, self.per)
        self.base, self.n = self.before + turns * self.per, 0


def wait_alone(eng, sem, value):
    eng.wait_ge(sem, value)
    eng.nop(nofuse=True)


def free_at_first(eng, *sems):
    for s in sems:
        eng.nop(nofuse=True).then_inc(s, 1)


def build(nc, x, edges, weights, firsts, early, late, out):
    tab = nc.dram_tensor("ln_table", (NP, D), F32, kind="Internal").ap()
    mtab = nc.dram_tensor("message_table", (2 * NP, D), F32, kind="Internal").ap()
    x1d = nc.dram_tensor("layer0_out", (NP, D), F32, kind="Internal").ap()

    with ExitStack() as ctx:
        def sb(name, shape, dt=F32):
            return ctx.enter_context(nc.sbuf_tensor(name, shape, dt))

        def sem(name):
            return ctx.enter_context(nc.semaphore(name))

        ps = ctx.enter_context(nc.psum_tensor("ps", [P, 8, 512], F32))
        early_sb = sb("early_sb", [P, NEARLY])
        late_sb = sb("late_sb", [P, NLATE])
        xh = sb("xh", [P, T, D])
        h0 = sb("h0", [P, T, D])
        h0t = sb("h0t", [P, 2, NP])
        nodes = sb("nodes", [P, 2, AGW])
        deg = sb("deg", [P, AGW])
        msg = sb("msg", [P, 2 * CH, D])
        oh = sb("oh", [P, 2 * CH, P])
        ohb = sb("ohb", [P, 2 * CH, P], BF16)
        ed = sb("ed", [P, GP, 3, CH], I32)
        ew = sb("ew", [P, GP, CH])
        st = sb("st", [P, 2, 3, CH], I32)
        stw = sb("stw", [P, 2, CH])
        bi = sb("bi", [P, GP], I32)
        ones = sb("ones", [P, P], BF16)
        onef = sb("onef", [P, 1])
        yb = sb("yb", [P, 2, BLK])
        lst = sb("lst", [P, NB, TB, 6])
        lm = sb("lm", [P, NB, 6, TB])
        zst = sb("zst", [P, 2, RUNS, 6])
        yst = sb("yst", [P, 2, RUNS, 6])
        bnv = sb("bnv", [P, 2, 2, 2])
        bns = sb("bns", [P, 2, 4, 2])
        bg = sb("bg", [P, 6])
        tmp = sb("tmp", [P, G * CH])
        tmp2 = sb("tmp2", [P, G * CH])
        cnt = sb("cnt", [P, 4])
        badi = sb("badi", [1, 1], I32)
        epsc = sb("epsc", [P, 1])
        woff = sb("woff", [P, 1])
        flat = h0t[:, :, :].rearrange("p h n -> p (h n)")
        r_sb = flat[:, 0:2 * BN].rearrange("p (h n) -> p h n", h=2)
        h1 = flat[:, 2 * BN:4 * BN].rearrange("p (t d) -> p t d", t=TB)
        h1t = sb("h1t", [P, 2, BN])
        hid = h0[:, 0:10, :].rearrange("p t d -> p (t d)").rearrange("p (r h n) -> p r h n", r=2, h=2)
        mst = h0[:, 10:20, :].rearrange("p (t r) d -> p t r d", r=2)
        at = 0

        def view(n, parts=P):
            nonlocal at
            at += n
            return flat[0:parts, at - n:at]

        gat = view(6 * BLK).rearrange("p (k n) -> p k n", k=6)
        cc = view(6 * BLK).rearrange("p (k h n) -> p k h n", k=3, h=2)
        mm1, mm2 = view(BLK), view(BLK)
        at = 8 * BN
        xb = view(2 * D, HB).rearrange("p (a d) -> p a d", a=2)
        ost = view(2 * D, HB).rearrange("p (a d) -> p a d", a=2)

        def col(name):
            if name in EARLY_COLS:
                return early_sb[:, slice(*EARLY_COLS[name])]
            return late_sb[:, slice(*LATE_COLS[name])]

        w1 = col("w1").rearrange("p (i o) -> p i o", i=2)
        w2 = col("w2").rearrange("p (i o) -> p i o", i=2)
        wrel = col("wrel").rearrange("p (r i o) -> p r i o", r=2, i=2)
        wih = col("wih").rearrange("p (i k o) -> p i k o", i=2, k=6)
        m1 = col("m1").rearrange("p (i o) -> p i o", i=2)
        m2, m3 = col("m2"), col("m3")
        brel = col("brel").rearrange("p (r h) -> p r h", r=2)
        brow = col("brow").rearrange("p (r d) -> p r d", r=2)
        ident, iota = col("ident"), col("iota")

        s_xin = [sem(f"s_xin{b}") for b in range(NB)]
        s_par, s_late, s_edge = sem("s_par"), sem("s_late"), sem("s_edge")
        s_dve, s_act = sem("s_dve"), sem("s_act")
        s_const, s_pool = sem("s_const"), sem("s_pool")
        s_lst, s_var, s_std, s_rstd, s_h0, s_tab = (sem(n) for n in ("s_lst", "s_var", "s_std", "s_rstd", "s_h0", "s_tab"))
        s_tr, s_h0t = sem("s_tr"), sem("s_h0t")
        s_st = [sem(f"s_st{h}") for h in range(2)]
        s_oh = [sem(f"s_oh{h}") for h in range(2)]
        s_slot = [sem(f"s_slot{k}") for k in range(2 * CH)]
        s_sum = [sem(f"s_sum{h}") for h in range(2)]
        s_add = [sem(f"s_add{h}") for h in range(2)]
        s_cnt, s_cntp, s_flag = sem("s_cnt"), sem("s_cntp"), sem("s_flag")
        zs = {n: sem("z_" + n) for n in ("yb", "mm", "cp", "st", "degm", "degs")}
        s_bn = [sem(f"s_bn{k}") for k in range(2)]
        s_bnv = [sem(f"s_bnv{k}") for k in range(2)]
        s_bnd = [sem(f"s_bnd{k}") for k in range(2)]
        s_hr = sem("s_hr")
        s_w2 = [sem(f"s_w2{k}") for k in range(2)]
        s_y = [sem(f"s_y{k}") for k in range(2)]
        s_r, s_ta, s_x1, s_var1, s_std1, s_rstd1, s_h1, s_tb, s_h1t = (
            sem(n) for n in ("s_r", "s_ta", "s_x1", "s_var1", "s_std1", "s_rstd1", "s_h1", "s_tb", "s_h1t"))
        s_l1, s_hid, s_l2, s_l2a, s_m, s_mtab, s_x1d, s_zero = (
            sem(n) for n in ("s_l1", "s_hid", "s_l2", "s_l2a", "s_m", "s_mtab", "s_x1d", "s_zero"))
        ms = {n: sem("m_" + n) for n in (
            "gmm", "gact", "c", "tc", "hn", "w1", "a1", "w2", "a2", "w3", "out", "xb", "st0", "st1")}
        g_slot = [sem(f"g_slot{c}") for c in range(CH)]
        g_st, g_oh, g_sum, g_add, g_off = (
            sem(n) for n in ("g_st", "g_oh", "g_sum", "g_add", "g_off"))

        def branch(eng, general, ordered):
            eng.wait_ge(s_flag, 1)
            outside = eng.value_load(badi[0:1, 0:1], min_val=0, max_val=1 << 17)
            with eng.If(outside > 0):
                general()
            with eng.Else():
                ordered()

        def row_moments(eng, own, k, var):
            me, mo, ve, vo = lst[:, k, :, 1], lst[:, k, :, 4], lst[:, k, :, 2], lst[:, k, :, 5]
            eng.tensor_tensor(lm[:, k, 0, :], me, mo, ALU.add)
            eng.tensor_tensor(lm[:, k, 1, :], me, mo, ALU.subtract)
            own.mark(eng.tensor_tensor(lm[:, k, 2, :], ve, vo, ALU.add))
            own.sync()
            eng.tensor_scalar(lm[:, k, 0:2, :], lm[:, k, 0:2, :], 0.5, None, ALU.mult)
            own.mark(eng.tensor_scalar(lm[:, k, 2, :], lm[:, k, 2, :], 1.0 / D, None, ALU.mult))
            own.sync()
            own.mark(eng.tensor_tensor(lm[:, k, 1, :], lm[:, k, 1, :], lm[:, k, 1, :], ALU.mult))
            own.sync()
            eng.tensor_tensor(lm[:, k, 2, :], lm[:, k, 2, :], lm[:, k, 1, :], ALU.add).then_inc(var, 1)

        def windows(eng, layer, group, window=None):
            with eng.Fori(0, T) as w:
                if window:
                    window(w)
                with eng.Fori(0, G) as g:
                    group(w, g, w * G + g + layer * T * G)

        block = ctx.enter_context(nc.Block())

        @block.sync
        def _(sp):
            for b in range(NB):
                sp.dma_start(xh[:, b * TB:(b + 1) * TB, :],
                             x[b * BN:(b + 1) * BN, :].rearrange("(t p) d -> p t d", p=P)).then_inc(s_xin[b], 16)
            sp.dma_start(ed[:, :, :, :], edges).then_inc(s_edge, 16)
            sp.dma_start(bi[:, :], firsts).then_inc(s_edge, 16)
            sp.dma_start(ew[:, :, :], weights).then_inc(s_edge, 16)
            for t, k in STORES:
                sp.wait_ge(s_h0, t + k)
                sp.dma_start(tab[t * P:(t + k) * P, :].rearrange("(t p) d -> p t d", p=P),
                             h0[:, t:t + k, :]).then_inc(s_tab, 16)
            sp.dma_start(late_sb[:, :], late).then_inc(s_late, 16)
            def store_x1(b):
                sp.wait_ge(s_x1, b + 1)
                sp.dma_start(x1d[ds(b * BN, BN), :].rearrange("(t p) d -> p t d", p=P),
                             xh[:, ds(b * TB, TB), :]).then_inc(s_x1d, 16)

            with sp.Fori(0, NB - 1) as b:
                store_x1(b)
                sp.wait_ge(s_m, (b + 1) * TB)
                for r in range(2):
                    sp.dma_start(mtab[ds(b * BN + r * NP, BN), :].rearrange("(t p) d -> p t d", p=P),
                                 mst[:, :, r, :]).then_inc(s_mtab, 16)
            store_x1(NB - 1)
            for t, k in LAST_STORES:
                sp.wait_ge(s_m, (NB - 1) * TB + t + k)
                for r in range(2):
                    sp.dma_start(mtab[r * NP + (NB - 1) * BN + t * P:r * NP + (NB - 1) * BN + (t + k) * P, :]
                                 .rearrange("(t p) d -> p t d", p=P), mst[:, t:t + k, r, :]).then_inc(s_mtab, 16)

            def load_rows(n):
                sp.dma_start(xb[:, :, :], x1d[ds(n * BLK, BLK), :].rearrange("(a p) d -> p a d", p=HB)
                             ).then_inc(ms["xb"], 16)

            sp.wait_ge(s_x1d, 16 * NB)
            with sp.Fori(0, RUNS - 1) as n:
                load_rows(n)
                sp.wait_ge(ms["out"], n + 1)
                sp.dma_start(out[ds(n * BLK, BLK), :].rearrange("(a p) d -> p a d", p=HB),
                             ost[:, :, :]).then_inc(ms["st0"], 16)
            load_rows(RUNS - 1)
            sp.wait_ge(ms["out"], RUNS)
            at = (RUNS - 1) * BLK
            sp.dma_start(out[at:at + HB, :], ost[:, 0, :]).then_inc(ms["st1"], 16)
            sp.dma_start(out[at + HB:N, :], ost[0:LASTH, 1, :]).then_inc(ms["st1"], 16)
            sp.wait_ge(ms["st0"], 16 * (RUNS - 1) + 1)
            sp.wait_ge(ms["st1"], 32)


        @block.gpsimd
        def _(pool):
            pool.memset(ones[:, :], 1.0)
            pool.memset(onef[:, :], 1.0)
            pool.memset(epsc[:, :], EPS)
            pool.memset(deg[:, :], 0.0).then_inc(s_const, 1)
            pool_own = Steps(pool, s_pool)
            for b in range(NB):
                pool.wait_ge(s_lst, b + 1)
                row_moments(pool, pool_own, b, s_var)

            def gathers(h, turn, table, row, written):
                pool.wait_ge(*written)
                wait_alone(pool, s_st[h], turn + 1)
                for c in range(CH):
                    pool.indirect_dma_start(
                        msg[:, h * CH + c, :], None, table,
                        bass.IndirectOffsetOnAxis(ap=st[:, h, row, c:c + 1], axis=0)
                    ).then_inc(s_slot[h * CH + c], 16)

            def gather_all(layer, table, written):
                def group(w, g, t):
                    pool.wait_ge(*written)
                    wait_alone(pool, g_st, t + 1)
                    for c in range(CH):
                        pool.indirect_dma_start(
                            msg[:, c, :], None, table,
                            bass.IndirectOffsetOnAxis(ap=st[:, 0, layer, c:c + 1], axis=0)).then_inc(g_slot[c], 16)
                windows(pool, layer, group)

            def gather_runs(layer, table, written):
                with pool.Fori(0, RUNS) as i:
                    for h in range(2):
                        gathers(h, i + (RUNS + 1 - h) * layer, table, layer, written)

            for layer, table, written in ((0, tab, (s_tab, 16 * len(STORES))), (1, mtab, (s_mtab, TABLE_STORED))):
                branch(pool, lambda: gather_all(layer, table, written), lambda: gather_runs(layer, table, written))

        @block.tensor
        def _(pe):
            pe.wait_ge(s_const, 1)
            pe.wait_ge(s_cnt, 1)
            pe.matmul(ps[0:1, 5, 0:1], cnt[:, 2:3], onef[:, :], start=True, stop=True).then_inc(s_cntp, 1)
            pe.wait_ge(s_par, 16)
            for t in range(T):
                pe.wait_ge(s_h0, t + 1)
                if t >= 2:
                    pe.wait_ge(s_h0t, t - 1)
                for h in range(2):
                    last = pe.transpose(ps[:, 3 + t % 2, h * P:(h + 1) * P], h0[:, t, h * P:(h + 1) * P], ident)
                last.then_inc(s_tr, 1)
            free_at_first(pe, s_y[0], s_y[1], s_l2a)

            def products(h, turn, layer, chunks):
                if chunks[0] == 0:
                    pe.wait_ge(s_oh[h], turn + (1 - h) * layer + 1)
                    pe.wait_ge(s_add[h], turn)
                last = chunk_products(h, layer, chunks, s_slot, turn * 16 + 16)
                if chunks[-1] == CH - 1:
                    last.then_inc(s_sum[h], 1)

            def chunk_products(h, layer, chunks, slots, landed):
                for c in chunks:
                    k = h * CH + c
                    pe.wait_ge(slots[k], landed)
                    pe.matmul(ps[:, h, 0:P], msg[:, k, 0:P], oh[:, k, :], start=(c == 0), stop=(c == CH - 1),
                              skip_group_check=True)
                    last = pe.matmul(ps[:, h, P:2 * P], msg[:, k, P:2 * P], oh[:, k, :], start=False,
                                     stop=(c == CH - 1), skip_group_check=True)
                    if layer == 0:
                        last = pe.matmul(ps[:, h, 2 * P:3 * P], ones[:, :], ohb[:, k, :], start=False,
                                         stop=(c == CH - 1), skip_group_check=True)
                return last

            def sum_all(layer):
                def group(w, g, t):
                    pe.wait_ge(g_oh, t + 1)
                    chunk_products(0, layer, range(CH), g_slot, t * 16 + 16).then_inc(g_sum, 1)
                windows(pe, layer, group)

            def z_mm(n, w):
                pe.wait_ge(zs["yb"], n + 1)
                for o in range(2):
                    for i in range(2):
                        last = pe.matmul(ps[:, 2, o * BLK:o * BLK + w], w1[:, i, o * P:(o + 1) * P], yb[:, i, 0:w],
                                         start=(i == 0), stop=(i == 1), skip_group_check=True)
                last.then_inc(zs["mm"], 1)

            early, late = list(range(6)), list(range(6, CH))

            def edge_loop(layer, dense):
                o = layer * RUNS
                full = early + late
                products(0, o, layer, full)
                products(1, o, layer, full)
                products(0, 1 + o, layer, full)
                pe.wait_ge(s_late, 16)
                with pe.Fori(1, RUNS - 1) as i:
                    dense(i - 1, BLK, lambda part: products(1, i + o, layer, part), i + o + 1, None)
                    products(0, i + o + 1, layer, full)
                dense(RUNS - 2, BLK, lambda part: products(1, RUNS - 1 + o, layer, part), RUNS + o, None)
                dense(RUNS - 1, LAST, None, RUNS + o, RUNS + o)

            def dense0(n, w, more, added_a, added_b):
                if more:
                    more(early)
                z_mm(n, w)
                if more:
                    more(late)

            def general0():
                sum_all(0)
                pe.wait_ge(s_late, 16)
                with pe.Fori(0, RUNS - 1) as n:
                    z_mm(n, BLK)
                z_mm(RUNS - 1, LAST)

            branch(pe, general0, lambda: edge_loop(0, dense0))

            def w2_mm(n, turn, k, w):
                pe.wait_ge(s_hr, n + 1)
                pe.wait_ge(s_y[k], turn + 1)
                for o in range(2):
                    for i in range(2):
                        last = pe.matmul(ps[:, 6 + k, o * BLK:o * BLK + w], w2[:, i, o * P:(o + 1) * P],
                                         nodes[:, i, ds(n * BLK, w)], start=(i == 0), stop=(i == 1),
                                         skip_group_check=True)
                last.then_inc(s_w2[k], 1)

            with pe.Fori(0, RUNS // 2 - 1) as j:
                for k in range(2):
                    w2_mm(j * 2 + k, j, k, BLK)
            w2_mm(RUNS - 2, RUNS // 2 - 1, 0, BLK)
            w2_mm(RUNS - 1, RUNS // 2 - 1, 1, LAST)

            def to_nodes(b):
                pe.wait_ge(s_r, b + 1)
                pe.wait_ge(s_h1t, b)
                for t in range(TB):
                    for h in range(2):
                        last = pe.transpose(ps[:, 3 + t // 2, (t % 2) * D + h * P:(t % 2) * D + (h + 1) * P],
                                            r_sb[:, h, t * P:(t + 1) * P], ident)
                last.then_inc(s_ta, 1)

            def to_features(b):
                pe.wait_ge(s_h1, b + 1)
                pe.wait_ge(s_x1, b + 1)
                for t in range(TB):
                    for h in range(2):
                        last = pe.transpose(ps[:, 3 + t // 2, (t % 2) * D + h * P:(t % 2) * D + (h + 1) * P],
                                            h1[:, t, h * P:(h + 1) * P], ident)
                last.then_inc(s_tb, 1)

            def first_mm(b):
                pe.wait_ge(s_h1t, b + 1)
                k = 0
                for r in range(2):
                    for o in range(2):
                        for c in range(2):
                            if k >= 2:
                                pe.wait_ge(s_hid, b * 8 + k - 1)
                            for i in range(2):
                                last = pe.matmul(ps[:, 6 + k % 2, 0:BN // 2], wrel[:, r, i, o * P:(o + 1) * P],
                                                 h1t[:, i, c * (BN // 2):(c + 1) * (BN // 2)],
                                                 start=(i == 0), stop=(i == 1))
                            last.then_inc(s_l1, 1)
                            k += 1

            def second_mm(b, tiles):
                for t in tiles:
                    pe.wait_ge(s_l2a, b * TB + (t - 1 if t >= 2 else 0) + 1)
                for r in range(2):
                    if tiles[0] == 0:
                        pe.wait_ge(s_hid, b * 8 + 4 * r + 4)
                    for t in tiles:
                        for i in range(2):
                            last = pe.matmul(ps[:, t % 2, r * D:(r + 1) * D], hid[:, r, i, t * P:(t + 1) * P],
                                             wrel[:, r, i, :], start=(i == 0), stop=(i == 1), skip_group_check=True)
                        if r == 1:
                            last.then_inc(s_l2, 1)

            to_nodes(0)
            to_features(0)
            with pe.Fori(0, NB - 1) as b:
                to_nodes(b + 1)
                first_mm(b)
                second_mm(b, [0, 1])
                to_features(b + 1)
                for t in (2, 3, 4):
                    second_mm(b, [t])
            first_mm(NB - 1)
            second_mm(NB - 1, [0, 1])
            for t in (2, 3, 4):
                second_mm(NB - 1, [t])

            def dense1(n, w, more, added_a, added_b):
                if more:
                    more([0])
                if added_a is not None:
                    pe.wait_ge(s_add[0], added_a)
                if added_b is not None:
                    pe.wait_ge(s_add[1], added_b)
                for k in range(6):
                    for i in range(2):
                        last = pe.matmul(ps[:, 3 + k // 2, (k % 2) * BLK:(k % 2) * BLK + w], wih[:, i, k, :],
                                         nodes[:, i, ds(n * BLK, w)], start=(i == 0), stop=(i == 1),
                                         skip_group_check=True)
                last.then_inc(ms["gmm"], 1)
                if more:
                    more([1, 2, 3, 4, 5])
                pe.wait_ge(ms["hn"], n + 1)
                for i in range(2):
                    last = pe.matmul(ps[:, 2, 0:w], m1[:, i, :], cc[:, 2, i, 0:w], start=(i == 0), stop=(i == 1),
                                     skip_group_check=True)
                last.then_inc(ms["w1"], 1)
                if more:
                    more([6, 7, 8])
                pe.wait_ge(ms["a1"], n + 1)
                pe.matmul(ps[:, 2, BLK:BLK + w], m2, mm1[:, 0:w], start=True, stop=True,
                          skip_group_check=True).then_inc(ms["w2"], 1)
                if more:
                    more([9, 10, 11, 12])
                pe.wait_ge(ms["a2"], n + 1)
                pe.matmul(ps[0:HB, 6, 0:D], mm2[:, 0:HB], m3, start=True, stop=True, skip_group_check=True)
                pe.matmul(ps[0:w - HB, 6, D:2 * D], mm2[:, HB:w], m3, start=True, stop=True,
                          skip_group_check=True).then_inc(ms["w3"], 1)

            def general1():
                sum_all(1)
                pe.wait_ge(g_add, 2 * T * G)
                with pe.Fori(0, RUNS - 1) as n:
                    dense1(n, BLK, None, None, None)
                dense1(RUNS - 1, LAST, None, None, None)

            branch(pe, general1, lambda: edge_loop(1, dense1))

        @block.scalar
        def _(act):
            act.dma_start(early_sb[:, :], early).then_inc(s_par, 16)
            act.wait_ge(s_const, 1)

            def spread(b, k, var, done, count):
                act.wait_ge(var, count)
                act.activation(lm[:, k, 3, :], lm[:, k, 2, :], ACT.Sqrt, bias=epsc[:, 0:1]).then_inc(done, 1)

            def normal0(b, tiles):
                for t in tiles:
                    act.activation(h0[:, b * TB + t, :], xh[:, b * TB + t, :], ACT.Relu,
                                   bias=lm[:, b, 5, t:t + 1], scale=lm[:, b, 4, t:t + 1]).then_inc(s_h0, 1)

            spread(0, 0, s_var, s_std, 1)
            for b in range(NB):
                act.wait_ge(s_rstd, b + 1)
                normal0(b, [0, 1, 2])
                if b + 1 < NB:
                    spread(b + 1, b + 1, s_var, s_std, b + 2)
                normal0(b, [3, 4])
            act.wait_ge(s_par, 16)
            for t in range(T):
                act.wait_ge(s_tr, t + 1)
                act.activation(h0t[:, :, t * P:(t + 1) * P],
                               ps[:, 3 + t % 2, 0:2 * P].rearrange("p (h n) -> p h n", h=2), ACT.Copy,
                               scale=col("eps")[:, 0:1]).then_inc(s_h0t, 1)

            def z_act(n, w):
                act.wait_ge(zs["degm"], n + 1)
                act.activation(deg[:, ds(n * BLK, w)], deg[:, ds(n * BLK, w)], ACT.Sqrt).then_inc(zs["degs"], 1)
                act.wait_ge(zs["mm"], n + 1)
                act.activation(nodes[:, :, ds(n * BLK, w)],
                               ps[:, 2, 0:2 * BLK].rearrange("p (h n) -> p h n", h=2)[:, :, 0:w],
                               ACT.Copy).then_inc(zs["cp"], 1)

            with act.Fori(0, RUNS - 1) as n:
                z_act(n, BLK)
            z_act(RUNS - 1, LAST)


            def bn_std(k):
                act.wait_ge(s_bnv[k], 1)
                act.activation(bns[:, k, 0, :], bnv[:, k, :, 1], ACT.Sqrt, bias=epsc[:, 0:1]).then_inc(s_bnd[k], 1)

            act.wait_ge(s_late, 16)
            bn_std(0)
            act.wait_ge(s_bn[0], 1)

            def relu_z(n, w):
                for h in range(2):
                    last = act.activation(nodes[:, h, ds(n * BLK, w)], nodes[:, h, ds(n * BLK, w)], ACT.Relu,
                                          bias=bns[:, 0, 3, h:h + 1], scale=bns[:, 0, 2, h:h + 1])
                last.then_inc(s_hr, 1)

            with act.Fori(0, RUNS - 1) as n:
                relu_z(n, BLK)
            relu_z(RUNS - 1, LAST)
            bn_std(1)
            act.wait_ge(s_bn[1], 1)

            def relu_y(b):
                act.wait_ge(s_ta, b)
                for h in range(2):
                    last = act.activation(r_sb[:, h, :], nodes[:, h, ds(b * BN, BN)], ACT.Relu,
                                          bias=bns[:, 1, 3, h:h + 1], scale=bns[:, 1, 2, h:h + 1])
                last.then_inc(s_r, 1)

            def normal1(b, tiles):
                if tiles[0] == 0:
                    act.wait_ge(s_rstd1, b + 1)
                    act.wait_ge(s_tb, b)
                for t in tiles:
                    last = act.activation(h1[:, t, :], xh[:, ds(b * TB + t, 1), :].rearrange("p a d -> p (a d)"),
                                          ACT.Relu, bias=lm[:, 0, 5, t:t + 1], scale=lm[:, 0, 4, t:t + 1])
                if tiles[-1] == TB - 1:
                    last.then_inc(s_h1, 1)

            def hidden(b, ks):
                for k in ks:
                    r, o, c = k // 4, k // 2 % 2, k % 2
                    act.wait_ge(s_l1, b * 8 + k + 1)
                    act.activation(hid[:, r, o, c * (BN // 2):(c + 1) * (BN // 2)], ps[:, 6 + k % 2, 0:BN // 2],
                                   ACT.Relu, bias=brel[:, r, o:o + 1]).then_inc(s_hid, 1)

            def message_relu(b):
                for t in range(TB):
                    act.wait_ge(s_l2a, b * TB + t + 2)
                    act.activation(mst[:, t, :, :], mst[:, t, :, :], ACT.Relu).then_inc(s_m, 1)

            relu_y(0)
            spread(0, 0, s_var1, s_std1, 1)
            normal1(0, list(range(TB)))
            relu_y(1)

            def message_turn(b, ahead):
                hidden(b, [0, 1, 2, 3, 4, 5])
                spread(b + 1, 0, s_var1, s_std1, b + 2)
                hidden(b, [6])
                normal1(b + 1, [0])
                hidden(b, [7])
                normal1(b + 1, [1, 2, 3, 4])
                if ahead:
                    relu_y(b + 2)
                message_relu(b)

            with act.Fori(0, NB - 2) as b:
                message_turn(b, True)
            message_turn(NB - 2, False)
            hidden(NB - 1, list(range(8)))
            message_relu(NB - 1)

            def mlp_act(n, w):
                act.wait_ge(ms["gmm"], n + 1)
                for k in range(6):
                    last = act.activation(gat[:, k, 0:w], ps[:, 3 + k // 2, (k % 2) * BLK:(k % 2) * BLK + w],
                                          ACT.Tanh if k in (2, 3) else ACT.Sigmoid, bias=bg[:, k:k + 1])
                last.then_inc(ms["gact"], 1)
                act.wait_ge(ms["c"], n + 1)
                act.activation(cc[:, 1, :, 0:w], cc[:, 0, :, 0:w], ACT.Tanh).then_inc(ms["tc"], 1)
                act.wait_ge(ms["w1"], n + 1)
                act.activation(mm1[:, 0:w], ps[:, 2, 0:w], ACT.Relu, bias=col("b1")).then_inc(ms["a1"], 1)
                act.wait_ge(ms["w2"], n + 1)
                act.activation(mm2[:, 0:w], ps[:, 2, BLK:BLK + w], ACT.Relu, bias=col("b2")).then_inc(ms["a2"], 1)

            with act.Fori(0, RUNS - 1) as n:
                mlp_act(n, BLK)
            mlp_act(RUNS - 1, LAST)

        @block.vector
        def _(dve):
            own = Steps(dve, s_dve)
            free_at_first(dve, s_mtab, ms["st0"])
            def row_scales(k, std, count, done):
                dve.wait_ge(std, count)
                own.mark(dve.reciprocal(lm[:, k, 4, :], lm[:, k, 3, :]))
                own.sync()
                dve.scalar_tensor_tensor(out=lm[:, k, 5, :], in0=lm[:, k, 0, :], scalar=-1.0, in1=lm[:, k, 4, :],
                                         op0=ALU.mult, op1=ALU.mult).then_inc(done, 1)

            for b in range(NB):
                dve.wait_ge(s_xin[b], 16)
                for t in range(TB):
                    last = dve.bn_stats(lst[:, b, t, :], xh[:, b * TB + t, :])
                last.then_inc(s_lst, 1)
                if b >= 1:
                    row_scales(b - 1, s_std, b, s_rstd)
            dve.wait_ge(s_edge, 48)
            dve.scalar_tensor_tensor(out=ed[:, :, 1, :], in0=ed[:, :, 1, :], scalar=float(NP), in1=ed[:, :, 0, :],
                                     op0=ALU.mult, op1=ALU.add)
            own.mark(dve.tensor_tensor(ed[:, :, 2, :].bitcast(F32), ed[:, :, 2, :],
                                       bi[:, :].rearrange("p (g o) -> p g o", o=1).broadcast_to([P, GP, CH]),
                                       ALU.subtract))
            row_scales(NB - 1, s_std, NB, s_rstd)
            rel = ed[:, 0:G, 2, :].bitcast(F32)
            dve.wait_ge(s_par, 16)
            own.sync()
            t1 = tmp[:, :].rearrange("p (g c) -> p g c", g=G)
            t2 = tmp2[:, :].rearrange("p (g c) -> p g c", g=G)
            own.mark(dve.tensor_scalar(t1, rel, 0.0, None, ALU.is_lt))
            own.sync()
            own.mark(dve.scalar_tensor_tensor(out=t2, in0=rel, scalar=float(P - 1), in1=t1, op0=ALU.is_gt,
                                              op1=ALU.add))
            own.sync()
            dve.reduce_sum(cnt[:, 0:1], tmp2[:, :], axis=AX_X)
            own.mark(dve.tensor_tensor(tmp[:, 0:G], bi[:, 0:G], col("lim"), ALU.is_lt))
            own.sync()
            own.mark(dve.reduce_sum(cnt[:, 1:2], tmp[:, 0:G], axis=AX_X))
            own.sync()
            dve.tensor_tensor(cnt[:, 2:3], cnt[:, 0:1], cnt[:, 1:2], ALU.add).then_inc(s_cnt, 1)
            dve.wait_ge(s_cntp, 1)
            dve.tensor_scalar(badi[:, :], ps[0:1, 5, 0:1], -float(NPAD), None, ALU.add).then_inc(s_flag, 1)

            def stage(h, turn, g, layer):
                if layer == 0:
                    dve.tensor_copy(stw[:, h, :], ew[:, ds(g, 1), :].rearrange("p a c -> p (a c)"))
                dve.tensor_copy(st[:, h, :, :], ed[:, ds(g, 1), :, :].rearrange("p a k c -> p (a k) c")
                                ).then_inc(s_st[h], 1)
                dve.wait_ge(s_st[h], turn + (1 - h) * layer + 1)
                one_hots(h, layer).then_inc(s_oh[h], 1)

            def one_hots(h, layer):
                rel = st[:, h, 2, :].bitcast(F32)
                for c in range(CH):
                    k = h * CH + c
                    if layer == 0:
                        dve.tensor_scalar(oh[:, k, :], iota[:, 0:P], rel[:, c:c + 1], stw[:, h, c:c + 1],
                                          ALU.is_equal, ALU.mult)
                        last = dve.tensor_scalar(ohb[:, k, :], iota[:, 0:P], rel[:, c:c + 1], None, ALU.is_equal)
                    else:
                        last = dve.tensor_scalar(oh[:, k, :], iota[:, 0:P], rel[:, c:c + 1], None, ALU.is_equal)
                return last

            def add(h, turn, g, layer):
                dve.wait_ge(s_sum[h], turn + 1)
                base = dve.value_load(bi[0:1, ds(g, 1)], min_val=0, max_val=N - 1)
                dve.wait_ge(s_add[1 - h], turn + h)
                if layer == 0:
                    dve.tensor_tensor(deg[:, ds(base, P)], deg[:, ds(base, P)], ps[:, h, 2 * P:3 * P], ALU.add)
                win = nodes[:, :, ds(base, P)]
                dve.tensor_tensor(win, win, ps[:, h, 0:2 * P].rearrange("p (h n) -> p h n", h=2), ALU.add
                                  ).then_inc(s_add[h], 1)

            def z_in(n, w, general=False):
                if general:
                    dve.wait_ge(g_add, T * G)
                elif w == BLK:
                    dve.wait_ge(s_add[0], n + 2)
                else:
                    dve.wait_ge(s_add[1], RUNS)
                dve.tensor_tensor(yb[:, :, 0:w], nodes[:, :, ds(n * BLK, w)], h0t[:, :, ds(n * BLK, w)],
                                  ALU.add).then_inc(zs["yb"], 1)
                d = deg[:, ds(n * BLK, w)]
                dve.tensor_scalar(d, d, 1.0, None, ALU.max).then_inc(zs["degm"], 1)

            def z_out(n, w, general=False):
                wait_alone(dve, zs["degs"], n + 1)
                d = deg[:, ds(n * BLK, w)]
                dve.reciprocal(d, d)
                wait_alone(dve, zs["cp"], n + 1)
                for h in range(2):
                    last = dve.bn_stats(zst[:, h, ds(n, 1), :].rearrange("p a s -> p (a s)"),
                                        nodes[:, h, ds(n * BLK, w)])
                last.then_inc(zs["st"], 1)

            def edge_loop(layer, before, after, per):
                o = layer * RUNS
                stage(0, o, 0, layer)
                stage(1, o, 1, layer)
                if layer == 0:
                    residual_and_biases()
                else:
                    dve.wait_ge(s_late, 16)
                add(0, o, 0, layer)
                stage(0, 1 + o, 2, layer)
                add(1, o, 1, layer)
                stage(1, 1 + o, 3, layer)
                add(0, 1 + o, 2, layer)
                stage(0, 2 + o, 4, layer)
                with dve.Fori(1, RUNS - 1) as i:
                    own.enter(i - 1, per)
                    before(i - 1, BLK)
                    add(1, i + o, i * 2 + 1, layer)
                    stage(1, i + o + 1, i * 2 + 3, layer)
                    after(i - 1, BLK)
                    add(0, i + o + 1, i * 2 + 2, layer)
                    stage(0, i + o + 2, i * 2 + 4, layer)
                    own.leave(RUNS - 2)
                before(RUNS - 2, BLK)
                if layer == 0:
                    after(RUNS - 2, BLK)
                add(1, RUNS - 1 + o, G - 1, layer)
                if layer == 1:
                    after(RUNS - 2, BLK)
                before(RUNS - 1, LAST)
                after(RUNS - 1, LAST)

            def general(layer, before, after):
                at_branch = own.base, own.n
                if layer == 0:
                    residual_and_biases()
                dve.memset(woff[:, :], -float(P)).then_inc(g_off, 1)

                def window(w):
                    dve.wait_ge(g_off, w + layer * (T + 1) + 1)
                    dve.tensor_scalar(woff[:, :], woff[:, :], float(P), None, ALU.add).then_inc(g_off, 1)
                    wait_alone(dve, g_off, w + layer * (T + 1) + 2)

                def group(w, g, t):
                    dve.tensor_copy(stw[:, 0, :], ew[:, ds(g, 1), :].rearrange("p a c -> p (a c)"))
                    dve.scalar_tensor_tensor(
                        out=st[:, 0, 2, :].bitcast(F32),
                        in0=ed[:, ds(g, 1), 2, :].rearrange("p a c -> p (a c)").bitcast(F32), scalar=woff[:, 0:1],
                        in1=bi[:, ds(g, 1)].broadcast_to([P, CH]), op0=ALU.subtract, op1=ALU.add)
                    dve.tensor_copy(st[:, 0, 0:2, :], ed[:, ds(g, 1), 0:2, :].rearrange("p a k c -> p (a k) c")
                                    ).then_inc(g_st, 1)
                    dve.wait_ge(g_st, t + 1)
                    one_hots(0, layer).then_inc(g_oh, 1)
                    dve.wait_ge(g_sum, t + 1)
                    if layer == 0:
                        d = deg[:, ds(w * P, P)]
                        dve.tensor_tensor(d, d, ps[:, 0, 2 * P:3 * P], ALU.add)
                    win = nodes[:, :, ds(w * P, P)]
                    dve.tensor_tensor(win, win, ps[:, 0, 0:2 * P].rearrange("p (h n) -> p h n", h=2), ALU.add
                                      ).then_inc(g_add, 1)
                    wait_alone(dve, g_add, t + 1)

                windows(dve, layer, group, window)
                with dve.Fori(0, RUNS - 1) as n:
                    own.enter(n, layer)
                    before(n, BLK, True)
                    after(n, BLK, True)
                    own.leave(RUNS - 1)
                before(RUNS - 1, LAST, True)
                after(RUNS - 1, LAST, True)
                own.base, own.n = at_branch

            def residual_and_biases():
                dve.memset(nodes[:, :, :], 0.0)
                dve.wait_ge(s_h0, T)
                for b in range(NB):
                    sl = slice(b * TB, (b + 1) * TB)
                    last = dve.tensor_tensor(xh[:, sl, :], xh[:, sl, :], h0[:, sl, :], ALU.add)
                own.mark(last)
                own.mark(dve.tensor_tensor(bg[:, :], col("bih"), col("bhh"), ALU.add))
                own.sync()

            branch(dve, lambda: general(0, z_in, z_out), lambda: edge_loop(0, z_in, z_out, 0))
            dve.wait_ge(zs["st"], RUNS)

            dve.wait_ge(s_late, 16)

            def bn_scales(k, stats, gamma, beta):
                own.sync()
                for h in range(2):
                    last = dve.bn_aggr(bnv[:, k, h, :], stats[:, h, :, :].rearrange("p r s -> p (r s)"))
                last.then_inc(s_bnv[k], 1)
                dve.wait_ge(s_bnd[k], 1)
                own.mark(dve.reciprocal(bns[:, k, 1, :], bns[:, k, 0, :]))
                own.sync()
                own.mark(dve.tensor_tensor(bns[:, k, 2, :], bns[:, k, 1, :], gamma, ALU.mult))
                own.sync()
                own.mark(dve.tensor_tensor(bns[:, k, 1, :], bnv[:, k, :, 0], bns[:, k, 2, :], ALU.mult))
                own.sync()
                dve.tensor_tensor(bns[:, k, 3, :], beta, bns[:, k, 1, :], ALU.subtract).then_inc(s_bn[k], 1)

            bn_scales(0, zst, col("g1"), col("be1"))

            def y_out(n, turn, k, w):
                dve.wait_ge(s_w2[k], turn + 1)
                both = ps[:, 6 + k, 0:2 * BLK].rearrange("p (h n) -> p h n", h=2)[:, :, 0:w]
                d = deg[:, ds(n * BLK, w)].rearrange("p (o n) -> p o n", o=1).broadcast_to([P, 2, w])
                dve.tensor_tensor(nodes[:, :, ds(n * BLK, w)], both, d, ALU.mult).then_inc(s_y[k], 1)

            def y_stats(n, turn, k, w):
                wait_alone(dve, s_y[k], turn + 2)
                for h in range(2):
                    last = dve.bn_stats(yst[:, h, ds(n, 1), :].rearrange("p a s -> p (a s)"),
                                        nodes[:, h, ds(n * BLK, w)])
                return last

            y_out(0, 0, 0, BLK)
            with dve.Fori(0, RUNS // 2 - 1) as j:
                for k in range(2):
                    y_out(j * 2 + k + 1, j + k, 1 - k, BLK)
                    y_stats(j * 2 + k, j, k, BLK)
            y_out(RUNS - 1, RUNS // 2 - 1, 1, LAST)
            y_stats(RUNS - 2, RUNS // 2 - 1, 0, BLK)
            own.mark(y_stats(RUNS - 1, RUNS // 2 - 1, 1, LAST))
            bn_scales(1, yst, col("gh"), col("beh"))

            banks = ((0, 2, 3), (2, 2, 4), (4, 1, 5))

            def residual(b):
                dve.wait_ge(s_ta, b + 1)
                for t, k, bank in banks:
                    rows = xh[:, ds(b * TB + t, k), :]
                    last = dve.tensor_tensor(rows, rows, ps[:, bank, 0:k * D].rearrange("p (t d) -> p t d", t=k),
                                             ALU.add)
                last.then_inc(s_x1, 1)
                dve.wait_ge(s_x1, b + 1)
                wait_alone(dve, s_h1, b)
                for t in range(TB):
                    last = dve.bn_stats(lst[:, 0, t, :], xh[:, ds(b * TB + t, 1), :].rearrange("p a d -> p (a d)"))
                own.mark(last)
                own.sync()
                row_moments(dve, own, 0, s_var1)
                row_scales(0, s_std1, b + 1, s_rstd1)

            def features(b):
                dve.wait_ge(s_tb, b + 1)
                for t, k, bank in banks:
                    last = dve.tensor_copy(
                        h1t[:, :, t * P:(t + k) * P].rearrange("p h (t n) -> p t h n", t=k),
                        ps[:, bank, 0:k * D].rearrange("p (t h n) -> p t h n", t=k, h=2))
                last.then_inc(s_h1t, 1)

            def message_bias(b, tiles):
                if tiles[0] == 0:
                    dve.wait_ge(s_mtab, b * 32 + 1)
                for t in tiles:
                    dve.wait_ge(s_l2, b * TB + t + 1)
                    dve.tensor_tensor(mst[:, t, :, :], ps[:, t % 2, :].rearrange("p (r d) -> p r d", r=2), brow,
                                      ALU.add).then_inc(s_l2a, 1)

            residual(0)
            features(0)
            with dve.Fori(0, NB - 1) as b:
                own.enter(b, 5)
                residual(b + 1)
                message_bias(b, [0, 1])
                features(b + 1)
                message_bias(b, [2, 3, 4])
                own.leave(NB - 1)
            dve.wait_ge(s_r, NB)
            own.mark(dve.memset(nodes[:, :, :], 0.0))
            message_bias(NB - 1, list(range(TB)))

            def mlp_in(n, w, general=False):
                dve.wait_ge(ms["gact"], n + 1)
                dve.tensor_tensor(cc[:, 0, :, 0:w], gat[:, 0:2, 0:w], gat[:, 2:4, 0:w], ALU.mult
                                  ).then_inc(ms["c"], 1)
                dve.wait_ge(ms["tc"], n + 1)
                dve.tensor_tensor(cc[:, 2, :, 0:w], gat[:, 4:6, 0:w], cc[:, 1, :, 0:w], ALU.mult
                                  ).then_inc(ms["hn"], 1)

            def mlp_out(n, w, general=False):
                dve.wait_ge(ms["w3"], n + 1)
                dve.wait_ge(ms["xb"], n * 16 + 16)
                dve.wait_ge(ms["st0"], n * 16 + 1)
                b3 = col("b3")
                for a, k in ((0, HB), (1, w - HB)):
                    last = dve.tensor_tensor(ost[0:k, a, :], ps[0:k, 6, a * D:(a + 1) * D], b3[0:k, :], ALU.add)
                own.mark(last)
                own.sync()
                for a, k in ((0, HB), (1, w - HB)):
                    last = dve.tensor_tensor(ost[0:k, a, :], ost[0:k, a, :], xb[0:k, a, :], ALU.add)
                last.then_inc(ms["out"], 1)

            branch(dve, lambda: general(1, mlp_in, mlp_out), lambda: edge_loop(1, mlp_in, mlp_out, 1))


def kernel(**inputs):
    import concourse.bacc as _bacc
    from concourse.bass_utils import run_bass_kernel_spmd as _run

    g = {k: np.asarray(v) for k, v in inputs.items()}

    def chunks(a, fill):
        full = np.full(GP * EG, fill, a.dtype)
        full[:E] = a
        return full.reshape(GP, CH, P).transpose(2, 0, 1)

    edges = np.stack([chunks(g["src"], 0), chunks(g["edge_type_2"], 0), chunks(g["dst"], -1)], axis=2)
    firsts = np.zeros(GP, np.int32)
    firsts[:G] = g["dst"][::EG]

    def halves(w):
        return np.ascontiguousarray(w.T).reshape(-1, P, w.shape[0]).transpose(1, 0, 2).reshape(P, -1)

    def cols(v):
        return v.reshape(-1, P).T

    used = [0, 1, 4, 5, 6, 7]
    wih = g["L1_gnn_W_ih"].reshape(8, P, D)[used].reshape(6 * P, D)
    pieces = {
        "w1": halves(g["L0_gnn_w1"]), "w2": halves(g["L0_gnn_w2"]),
        "wrel": np.concatenate([halves(g["L1_gnn_W_rel"][r]) for r in range(2)], axis=1),
        "wih": halves(wih), "m1": halves(g["L1_gnn_W1"]), "m2": halves(g["L1_gnn_W2"]), "m3": halves(g["L1_gnn_W3"]),
        "g1": cols(g["L0_gnn_gamma1"]), "be1": cols(g["L0_gnn_beta1"]),
        "gh": cols(g["L0_gnn_gamma_h"]), "beh": cols(g["L0_gnn_beta_h"]), "brel": cols(g["L1_gnn_b_rel"]),
        "bih": cols(g["L1_gnn_b_ih"])[:, used], "bhh": cols(g["L1_gnn_b_hh"])[:, used],
        "b1": cols(g["L1_gnn_b1"]), "b2": cols(g["L1_gnn_b2"]),
        "eps": np.broadcast_to(g["L0_gnn_eps_weight"][None], (P, 1)),
        "brow": np.broadcast_to(g["L1_gnn_b_rel"].reshape(1, -1), (P, 2 * D)),
        "b3": np.broadcast_to(g["L1_gnn_b3"][None], (P, D)),
        "ident": np.eye(P, dtype=np.float32),
        "iota": np.broadcast_to(np.arange(P, dtype=np.float32), (P, P)),
        "lim": np.broadcast_to(np.array([max(k - 1, 0) // 2 * BLK for k in range(G)], np.float32), (P, G)),
    }
    def packed(cols, n):
        a = np.zeros((P, n), np.float32)
        for name, (i, j) in cols.items():
            a[:, i:j] = pieces[name]
        return a

    x = np.zeros((NP, D), np.float32)
    x[:N] = g["x"]
    arrays = {
        "x": x,
        "edges": np.ascontiguousarray(edges.astype(np.int32)),
        "weights": np.ascontiguousarray(chunks(g["edge_weight"], 0)),
        "firsts": np.ascontiguousarray(np.broadcast_to(firsts, (P, GP))),
        "early": packed(EARLY_COLS, NEARLY),
        "late": packed(LATE_COLS, NLATE),
    }
    nc = _bacc.Bacc("TRN2", target_bir_lowering=False, num_devices=1)
    args = [nc.dram_tensor("in_" + n, a.shape, mybir.dt.from_np(a.dtype), kind="ExternalInput").ap()
            for n, a in arrays.items()]
    out = nc.dram_tensor("out", (N, D), F32, kind="ExternalOutput").ap()
    build(nc, *args, out)
    r = _run(nc, [{"in_" + n: a for n, a in arrays.items()}], core_ids=[0])
    return r.results[0]["out"]
```

```python
from contextlib import ExitStack

import numpy as np

import concourse.bass as bass
from concourse import mybir

F32 = mybir.dt.float32
BF16 = mybir.dt.bfloat16
F32R = mybir.dt.float32r
I32 = mybir.dt.int32
ALU = mybir.AluOpType
ACT = mybir.ActivationFunctionType
AX_X = mybir.AxisListType.X
ds = bass.ds

P = 128
N = 3125
D = 256
E = 53125
CH = 13
G = 32
EG = CH * P
NPAD = G * EG - E
T = 25
TB = 5
NB = T // TB
BN = TB * P
NP = T * P
STORES = [(b * TB, TB) for b in range(NB - 1)] + [(T - TB, TB - 2), (T - 2, 2)]
LAST_STORES = ((0, 2), (2, 2), (4, 1))
TABLE_STORED = 32 * (NB - 1 + len(LAST_STORES)) + 1
PARTS = ((0, 2), (2, TB))
CHUNKS = tuple((a * P, b * P) for a, b in PARTS)
RUNS = G // 2
BLK = 200
LAST = N - (RUNS - 1) * BLK
HB = BLK // 2
AGW = N + P + 11
EPS = 1e-5
assert LAST <= P
assert NPAD >= 0 and RUNS * BLK >= N and AGW >= N + P and T * P >= N

EARLY = (("eps", 1), ("ident", P), ("iota", P), ("lim", G), ("bih", 6), ("bhh", 6))
LATE = (
    ("w1", 2 * D), ("w2", 2 * D), ("wrel", 4 * D), ("wih", 2 * 6 * P), ("m1", 2 * P), ("m2", P), ("m3", D),
    ("g1", 2), ("be1", 2), ("gh", 2), ("beh", 2), ("brel", 4), ("b1", 1), ("b2", 1), ("brow", 2 * D), ("b3", D),
)


def columns(names):
    out, at = {}, 0
    for name, n in names:
        out[name] = (at, at + n)
        at += n
    return out, at


EARLY_COLS, NEARLY = columns(EARLY)
LATE_COLS, NLATE = columns(LATE)


class Steps:

    def __init__(self, eng, sem):
        self.eng, self.sem, self.base, self.n = eng, sem, 0, 0

    def mark(self, ins):
        ins.then_inc(self.sem, 1)
        self.n += 1

    def sync(self):
        self.eng.wait_ge(self.sem, self.base + self.n)

    def enter(self, turn, per):
        self.before = self.base + self.n
        self.per = per
        self.base, self.n = turn * per + self.before, 0

    def leave(self, turns):
        assert self.n == self.per, (self.n, self.per)
        self.base, self.n = self.before + turns * self.per, 0


def pieces(w):
    return ((0, HB), (HB, w - HB)) if w > P else ((0, w),)


def wait_alone(eng, sem, value):
    eng.wait_ge(sem, value)
    eng.nop(nofuse=True)


def free_at_first(eng, *sems):
    for s in sems:
        eng.nop(nofuse=True).then_inc(s, 1)


def build(nc, x, edges, weights, firsts, early, late, out):
    tab = nc.dram_tensor("ln_table", (NP, D), F32, kind="Internal").ap()
    mtab = nc.dram_tensor("message_table", (2 * NP, D), F32, kind="Internal").ap()
    x1d = nc.dram_tensor("layer0_out", (NP, D), F32, kind="Internal").ap()

    with ExitStack() as ctx:
        def sb(name, shape, dt=F32):
            return ctx.enter_context(nc.sbuf_tensor(name, shape, dt))

        def sem(name):
            return ctx.enter_context(nc.semaphore(name))

        ps = ctx.enter_context(nc.psum_tensor("ps", [P, 8, 512], F32))
        early_sb = sb("early_sb", [P, NEARLY])
        late_sb = sb("late_sb", [P, NLATE])
        xh = sb("xh", [P, T, D])
        h0 = sb("h0", [P, T, D])
        h0t = sb("h0t", [P, 2, NP])
        nodes = sb("nodes", [P, 2, AGW])
        deg = sb("deg", [P, AGW])
        ohb = sb("ohb", [P, 2 * CH, P], BF16)
        ed = sb("ed", [P, G, 3, CH], I32)
        ew = sb("ew", [P, G, CH])
        st = sb("st", [P, 2, 3, CH], I32)
        stw = sb("stw", [P, 2, CH])
        bi = sb("bi", [P, G], I32)
        ones = sb("ones", [P, P], BF16)
        onef = sb("onef", [P, 1])
        yb = sb("yb", [P, 2, BLK])
        lst = sb("lst", [P, NB, TB, 6])
        lm = sb("lm", [P, NB, 6, TB])
        raw_idx = sb("raw_idx", [P, CH], I32)
        raw_st = sb("raw_st", [P, 1, CH, 6])
        raw_lm = sb("raw_lm", [P, 1, 6, CH])
        zst = sb("zst", [P, 2, RUNS, 6])
        yst = sb("yst", [P, 2, RUNS, 6])
        bnv = sb("bnv", [P, 2, 2, 2])
        bns = sb("bns", [P, 2, 4, 2])
        bg = sb("bg", [P, 6])
        tmp = sb("tmp", [P, G * CH])
        tmp2 = sb("tmp2", [P, G * CH])
        cnt = sb("cnt", [P, 4])
        badi = sb("badi", [1, 1], I32)
        epsc = sb("epsc", [P, 1])
        woff = sb("woff", [P, 1])
        flat = h0t[:, :, :].rearrange("p h n -> p (h n)")
        r_sb = flat[:, 0:2 * BN].rearrange("p (h n) -> p h n", h=2)
        h1 = flat[:, 2 * BN:4 * BN].rearrange("p (t d) -> p t d", t=TB)
        hid = h0[:, 0:10, :].rearrange("p t d -> p (t d)").rearrange("p (r h n) -> p r h n", r=2, h=2)
        mst = h0[:, 10:20, :].rearrange("p (t r) d -> p t r d", r=2)
        at = 0

        def view(n, parts=P):
            nonlocal at
            at += n
            return flat[0:parts, at - n:at]

        gat = view(6 * BLK).rearrange("p (k n) -> p k n", k=6)
        cc = view(6 * BLK).rearrange("p (k h n) -> p k h n", k=3, h=2)
        mm1, mm2 = view(BLK), view(BLK)
        at = 8 * BN
        xb = view(2 * D).rearrange("p (a d) -> p a d", a=2)
        ost = view(2 * D).rearrange("p (a d) -> p a d", a=2)

        def col(name):
            if name in EARLY_COLS:
                return early_sb[:, slice(*EARLY_COLS[name])]
            return late_sb[:, slice(*LATE_COLS[name])]

        w1 = col("w1").rearrange("p (i o) -> p i o", i=2)
        w2 = col("w2").rearrange("p (i o) -> p i o", i=2)
        wrel = col("wrel").rearrange("p (r i o) -> p r i o", r=2, i=2)
        wih = col("wih").rearrange("p (i k o) -> p i k o", i=2, k=6)
        m1 = col("m1").rearrange("p (i o) -> p i o", i=2)
        m2, m3 = col("m2"), col("m3")
        brel = col("brel").rearrange("p (r h) -> p r h", r=2)
        brow = col("brow").rearrange("p (r d) -> p r d", r=2)
        ident, iota = col("ident"), col("iota")

        with ExitStack() as shared:
            msg = shared.enter_context(nc.sbuf_tensor("msg", [P, 2 * CH, D], F32))
            oh = shared.enter_context(nc.sbuf_tensor("oh", [P, 2 * CH, P], F32))
        wrel_up, wrel_lo = (sb(n, [P, 2, 2, D], F32R) for n in ("wrel_up", "wrel_lo"))
        h1t_up, h1t_lo = (sb(n, [P, 2, BN], F32R) for n in ("h1t_up", "h1t_lo"))
        assert 2 * (4 * D + 2 * BN) <= 2 * CH * (D + P)

        s_xin = [sem(f"s_xin{b}") for b in range(NB)]
        s_par, s_late, s_edge = sem("s_par"), sem("s_late"), sem("s_edge")
        s_dve = sem("s_dve")
        s_const, s_sums0 = sem("s_const"), sem("s_sums0")
        r_idx, r_var, r_std, r_rstd, r_norm = (sem(n) for n in ("r_idx", "r_var", "r_std", "r_rstd", "r_norm"))
        r_oh = sem("r_oh")
        s_xh = sem("s_xh")
        s_wrel, s_h1u = sem("s_wrel"), sem("s_h1u")
        s_var, s_std, s_rstd, s_h0, s_tab = (sem(n) for n in ("s_var", "s_std", "s_rstd", "s_h0", "s_tab"))
        s_tr, s_h0t = sem("s_tr"), sem("s_h0t")
        s_st = [sem(f"s_st{h}") for h in range(2)]
        s_oh = [sem(f"s_oh{h}") for h in range(2)]
        s_slot = [sem(f"s_slot{k}") for k in range(2 * CH)]
        s_sum = [sem(f"s_sum{h}") for h in range(2)]
        s_add = [sem(f"s_add{h}") for h in range(2)]
        s_cnt, s_cntp, s_flag = sem("s_cnt"), sem("s_cntp"), sem("s_flag")
        zs = {n: sem("z_" + n) for n in ("yb", "mm", "cp", "st", "degm", "degs")}
        s_bn = [sem(f"s_bn{k}") for k in range(2)]
        s_bnv = [sem(f"s_bnv{k}") for k in range(2)]
        s_bnd = [sem(f"s_bnd{k}") for k in range(2)]
        s_hr = sem("s_hr")
        s_w2 = [sem(f"s_w2{k}") for k in range(2)]
        s_y = [sem(f"s_y{k}") for k in range(2)]
        s_r, s_ta, s_x1, s_var1, s_std1, s_rstd1, s_h1, s_tb, s_h1t = (
            sem(n) for n in ("s_r", "s_ta", "s_x1", "s_var1", "s_std1", "s_rstd1", "s_h1", "s_tb", "s_h1t"))
        s_l1, s_hid, s_l2, s_l2a, s_m, s_mtab, s_x1d = (
            sem(n) for n in ("s_l1", "s_hid", "s_l2", "s_l2a", "s_m", "s_mtab", "s_x1d"))
        ms = {n: sem("m_" + n) for n in (
            "gmm", "gact", "c", "tc", "hn", "w1", "a1", "w2", "a2", "w3", "out", "xb", "st0", "st1")}
        g_slot = [sem(f"g_slot{c}") for c in range(CH)]
        g_st, g_oh, g_sum, g_add, g_off = (
            sem(n) for n in ("g_st", "g_oh", "g_sum", "g_add", "g_off"))

        def branch(eng, general, ordered):
            eng.wait_ge(s_flag, 1)
            outside = eng.value_load(badi[0:1, 0:1], min_val=0, max_val=1 << 17)
            with eng.If(outside > 0):
                general()
            with eng.Else():
                ordered()

        def signals(b, part):
            return b + 2 if part is None else part + 1

        def tiles_of(part):
            return (0, TB) if part is None else PARTS[part]

        banks = ((0, 2, 3), (2, 2, 4), (4, 1, 5))

        def banks_of(part):
            return banks if part is None else (banks[0:1], banks[1:3])[part]

        def in_tiles(buffer, t, k):
            return buffer[:, :, t * P:(t + k) * P].rearrange("p h (t n) -> p t h n", t=k)

        def in_bank(bank, k):
            return ps[:, bank, 0:k * D].rearrange("p (t h n) -> p t h n", t=k, h=2)

        def windows(eng, layer, group, window=None):
            with eng.Fori(0, T) as w:
                if window:
                    window(w)
                with eng.Fori(0, G) as g:
                    group(w, g, w * G + g + layer * T * G)

        block = ctx.enter_context(nc.Block())

        @block.sync
        def _(sp):
            for b in range(NB):
                sp.dma_start(xh[:, b * TB:(b + 1) * TB, :],
                             x[b * BN:(b + 1) * BN, :].rearrange("(t p) d -> p t d", p=P)).then_inc(s_xin[b], 16)
            sp.dma_start(ed[:, :, :, :], edges).then_inc(s_edge, 16)
            sp.dma_start(bi[:, :], firsts).then_inc(s_edge, 16)
            sp.dma_start(ew[:, :, :], weights).then_inc(s_edge, 16)
            for t, k in STORES:
                sp.wait_ge(s_h0, t + k)
                sp.dma_start(tab[t * P:(t + k) * P, :].rearrange("(t p) d -> p t d", p=P),
                             h0[:, t:t + k, :]).then_inc(s_tab, 16)
            sp.dma_start(late_sb[:, :], late).then_inc(s_late, 16)
            def store_x1(b):
                sp.wait_ge(s_x1, signals(b, None))
                sp.dma_start(x1d[ds(b * BN, BN), :].rearrange("(t p) d -> p t d", p=P),
                             xh[:, ds(b * TB, TB), :]).then_inc(s_x1d, 16)

            with sp.Fori(0, NB - 1) as b:
                store_x1(b)
                sp.wait_ge(s_m, (b + 1) * TB)
                for r in range(2):
                    sp.dma_start(mtab[ds(b * BN + r * NP, BN), :].rearrange("(t p) d -> p t d", p=P),
                                 mst[:, :, r, :]).then_inc(s_mtab, 16)
            store_x1(NB - 1)
            for t, k in LAST_STORES:
                sp.wait_ge(s_m, (NB - 1) * TB + t + k)
                for r in range(2):
                    sp.dma_start(mtab[r * NP + (NB - 1) * BN + t * P:r * NP + (NB - 1) * BN + (t + k) * P, :]
                                 .rearrange("(t p) d -> p t d", p=P), mst[:, t:t + k, r, :]).then_inc(s_mtab, 16)

            def load_rows(n):
                sp.dma_start(xb[0:HB, :, :], x1d[ds(n * BLK, BLK), :].rearrange("(a p) d -> p a d", p=HB)
                             ).then_inc(ms["xb"], 16)

            sp.wait_ge(s_x1d, 16 * NB)
            with sp.Fori(0, RUNS - 1) as n:
                load_rows(n)
                sp.wait_ge(ms["out"], n + 1)
                sp.dma_start(out[ds(n * BLK, BLK), :].rearrange("(a p) d -> p a d", p=HB),
                             ost[0:HB, :, :]).then_inc(ms["st0"], 16)
            at = (RUNS - 1) * BLK
            sp.dma_start(xb[0:LAST, 0, :], x1d[at:N, :]).then_inc(ms["xb"], 16)
            sp.wait_ge(ms["out"], RUNS)
            sp.dma_start(out[at:N, :], ost[0:LAST, 0, :]).then_inc(ms["st1"], 16)
            sp.wait_ge(ms["st0"], 16 * (RUNS - 1) + 1)
            sp.wait_ge(ms["st1"], 16)


        @block.gpsimd
        def _(pool):
            pool.memset(ones[:, :], 1.0)
            pool.memset(onef[:, :], 1.0)
            pool.memset(epsc[:, :], EPS).then_inc(s_const, 1)
            wait_alone(pool, r_idx, 16)
            for c in range(CH):
                pool.indirect_dma_start(
                    msg[:, c, :], None, x,
                    bass.IndirectOffsetOnAxis(ap=raw_idx[:, c:c + 1], axis=0)).then_inc(s_slot[c], 16)
            pool.memset(deg[:, :], 0.0)
            pool.memset(nodes[:, :, :], 0.0).then_inc(s_sums0, 1)
            tab_stored = (s_tab, 16 * len(STORES))
            mtab_stored = (s_mtab, TABLE_STORED)

            def gathers(h, turn, table, row, written):
                pool.wait_ge(*written)
                wait_alone(pool, s_st[h], turn + 1)
                for c in range(CH):
                    pool.indirect_dma_start(
                        msg[:, h * CH + c, :], None, table,
                        bass.IndirectOffsetOnAxis(ap=st[:, h, row, c:c + 1], axis=0)
                    ).then_inc(s_slot[h * CH + c], 16)

            def gather_all(layer, table, written):
                pool.wait_ge(r_norm, CH)

                def group(w, g, t):
                    pool.wait_ge(*written)
                    wait_alone(pool, g_st, t + 1)
                    for c in range(CH):
                        pool.indirect_dma_start(
                            msg[:, c, :], None, table,
                            bass.IndirectOffsetOnAxis(ap=st[:, 0, layer, c:c + 1], axis=0)).then_inc(g_slot[c], 16)
                windows(pool, layer, group)

            def gather_runs(layer, table, written):
                if layer == 0:
                    gathers(1, 0, table, layer, written)
                with pool.Fori(1 - layer, RUNS) as i:
                    for h in range(2):
                        gathers(h, i + RUNS * layer, table, layer, written)

            branch(pool, lambda: gather_all(0, tab, tab_stored), lambda: gather_runs(0, tab, tab_stored))
            pool.wait_ge(s_h0, T)
            for b in range(NB):
                sl = slice(b * TB, (b + 1) * TB)
                pool.tensor_tensor(xh[:, sl, :], xh[:, sl, :], h0[:, sl, :], ALU.add).then_inc(s_xh, 1)
            pool.wait_ge(s_r, signals(NB - 1, None))
            pool.memset(nodes[:, :, :], 0.0).then_inc(s_sums0, 1)
            branch(pool, lambda: gather_all(1, mtab, mtab_stored), lambda: gather_runs(1, mtab, mtab_stored))

        @block.tensor
        def _(pe):
            pe.wait_ge(s_const, 1)
            pe.wait_ge(s_cnt, 1)
            pe.matmul(ps[0:1, 5, 0:1], cnt[:, 2:3], onef[:, :], start=True, stop=True).then_inc(s_cntp, 1)
            pe.wait_ge(s_par, 16)
            eps_banks = (3, 4, 6, 7)

            def eps_term():
                pe.wait_ge(s_h0, T)
                for t in range(T):
                    if t >= len(eps_banks):
                        pe.wait_ge(s_h0t, t - len(eps_banks) + 1)
                    for h in range(2):
                        last = pe.transpose(ps[:, eps_banks[t % 4], h * P:(h + 1) * P], h0[:, t, h * P:(h + 1) * P],
                                            ident)
                    last.then_inc(s_tr, 1)

            free_at_first(pe, s_y[0], s_y[1], s_l2a)

            def products(h, turn, layer, chunks, first=False):
                if chunks[0] == 0:
                    if not first:
                        pe.wait_ge(s_oh[h], turn + 1)
                    pe.wait_ge(s_add[h], turn)
                last = chunk_products(h, layer, chunks, s_slot, turn * 16 + 16, first)
                if chunks[-1] == CH - 1:
                    last.then_inc(s_sum[h], 1)

            def chunk_products(h, layer, chunks, slots, landed, first=False):
                for c in chunks:
                    k = h * CH + c
                    pe.wait_ge(slots[k], landed)
                    if first:
                        pe.wait_ge(r_oh, k + 1)
                        if h == 0:
                            pe.wait_ge(r_norm, c + 1)
                    pe.matmul(ps[:, h, 0:P], msg[:, k, 0:P], oh[:, k, :], start=(c == 0), stop=(c == CH - 1),
                              skip_group_check=True)
                    last = pe.matmul(ps[:, h, P:2 * P], msg[:, k, P:2 * P], oh[:, k, :], start=False,
                                     stop=(c == CH - 1), skip_group_check=True)
                    if layer == 0:
                        last = pe.matmul(ps[:, h, 2 * P:3 * P], ones[:, :], ohb[:, k, :], start=False,
                                         stop=(c == CH - 1), skip_group_check=True)
                return last

            def sum_all(layer):
                def group(w, g, t):
                    pe.wait_ge(g_oh, t + 1)
                    chunk_products(0, layer, range(CH), g_slot, t * 16 + 16).then_inc(g_sum, 1)
                windows(pe, layer, group)

            def z_mm(n, w):
                pe.wait_ge(zs["yb"], n + 1)
                for o in range(2):
                    for i in range(2):
                        last = pe.matmul(ps[:, 2, o * BLK:o * BLK + w], w1[:, i, o * P:(o + 1) * P], yb[:, i, 0:w],
                                         start=(i == 0), stop=(i == 1), skip_group_check=True)
                last.then_inc(zs["mm"], 1)

            early, late = list(range(6)), list(range(6, CH))

            def edge_loop(layer, dense):
                o = layer * RUNS
                full = early + late
                products(0, o, layer, full, layer == 0)
                products(1, o, layer, full, layer == 0)
                if layer == 0:
                    eps_term()
                products(0, 1 + o, layer, full)
                pe.wait_ge(s_late, 16)
                with pe.Fori(1, RUNS - 1) as i:
                    dense(i - 1, BLK, lambda part: products(1, i + o, layer, part), i + o + 1, None)
                    products(0, i + o + 1, layer, full)
                dense(RUNS - 2, BLK, lambda part: products(1, RUNS - 1 + o, layer, part), RUNS + o, None)
                dense(RUNS - 1, LAST, None, RUNS + o, RUNS + o)

            def dense0(n, w, more, added_a, added_b):
                if more:
                    more(early)
                z_mm(n, w)
                if more:
                    more(late)

            def general0():
                eps_term()
                sum_all(0)
                pe.wait_ge(s_late, 16)
                with pe.Fori(0, RUNS - 1) as n:
                    z_mm(n, BLK)
                z_mm(RUNS - 1, LAST)

            branch(pe, general0, lambda: edge_loop(0, dense0))

            def w2_mm(n, turn, k, w):
                pe.wait_ge(s_hr, n + 1)
                pe.wait_ge(s_y[k], turn + 1)
                for o in range(2):
                    for i in range(2):
                        last = pe.matmul(ps[:, 6 + k, o * BLK:o * BLK + w], w2[:, i, o * P:(o + 1) * P],
                                         nodes[:, i, ds(n * BLK, w)], start=(i == 0), stop=(i == 1),
                                         skip_group_check=True)
                last.then_inc(s_w2[k], 1)

            with pe.Fori(0, RUNS // 2 - 1) as j:
                for k in range(2):
                    w2_mm(j * 2 + k, j, k, BLK)
            w2_mm(RUNS - 2, RUNS // 2 - 1, 0, BLK)
            w2_mm(RUNS - 1, RUNS // 2 - 1, 1, LAST)

            def to_nodes(b, part=None):
                pe.wait_ge(s_r, signals(b, part))
                if part is None:
                    pe.wait_ge(s_h1t, signals(b - 1, None))
                for t in range(*tiles_of(part)):
                    for h in range(2):
                        last = pe.transpose(ps[:, 3 + t // 2, (t % 2) * D + h * P:(t % 2) * D + (h + 1) * P],
                                            r_sb[:, h, t * P:(t + 1) * P], ident)
                last.then_inc(s_ta, 1)

            def to_features(b, part=None):
                pe.wait_ge(s_h1, signals(b, part))
                pe.wait_ge(s_x1, signals(b, part))
                for t in range(*tiles_of(part)):
                    for h in range(2):
                        last = pe.transpose(ps[:, 3 + t // 2, (t % 2) * D + h * P:(t % 2) * D + (h + 1) * P],
                                            h1[:, t, h * P:(h + 1) * P], ident)
                last.then_inc(s_tb, 1)

            def split_mm(to, left, right):
                terms = [(a[u], b[v])
                         for a, b in zip(left, right) for u, v in ((0, 0), (0, 1), (1, 0))]
                for n, (a, b) in enumerate(terms):
                    last = pe.matmul(to, a, b, start=(n == 0), stop=(n == len(terms) - 1), skip_group_check=True)
                return last

            def first_mm(b, c, part=None, which=range(4)):
                pe.wait_ge(s_h1t, signals(b, part))
                lo, hi = CHUNKS[c]
                for q in which:
                    r, o, k = q // 2, q % 2, 4 * c + q
                    if k >= 2:
                        pe.wait_ge(s_hid, b * 8 + k - 1)
                    cols = slice(o * P, (o + 1) * P)
                    split_mm(ps[:, 6 + k % 2, 0:hi - lo],
                             [(wrel_up[:, r, i, cols], wrel_lo[:, r, i, cols]) for i in range(2)],
                             [(h1t_up[:, i, lo:hi], h1t_lo[:, i, lo:hi]) for i in range(2)]).then_inc(s_l1, 1)

            def second_mm(b, tiles):
                for t in tiles:
                    pe.wait_ge(s_hid, b * 8 + (8 if t >= PARTS[1][0] else 4))
                    pe.wait_ge(s_l2a, b * TB + (t - 1 if t >= 2 else 0) + 1)
                    for r in range(2):
                        for i in range(2):
                            last = pe.matmul(ps[:, t % 2, r * D:(r + 1) * D], hid[:, r, i, t * P:(t + 1) * P],
                                             wrel[:, r, i, :], start=(i == 0), stop=(i == 1), skip_group_check=True)
                    last.then_inc(s_l2, 1)

            to_nodes(0, 0)
            to_nodes(0, 1)
            pe.wait_ge(s_wrel, 1)
            to_features(0, 0)
            first_mm(0, 0, 0, (0, 1))
            to_features(0, 1)
            first_mm(0, 0, 0, (2, 3))
            with pe.Fori(0, NB - 1) as b:
                to_nodes(b + 1)
                first_mm(b, 1)
                second_mm(b, [0, 1, 2])
                to_features(b + 1)
                second_mm(b, [3, 4])
                first_mm(b + 1, 0)
            first_mm(NB - 1, 1)
            second_mm(NB - 1, range(TB))

            def dense1(n, w, more, added_a, added_b):
                if more:
                    more([0])
                if added_a is not None:
                    pe.wait_ge(s_add[0], added_a)
                if added_b is not None:
                    pe.wait_ge(s_add[1], added_b)
                for k in range(6):
                    for i in range(2):
                        last = pe.matmul(ps[:, 3 + k // 2, (k % 2) * BLK:(k % 2) * BLK + w], wih[:, i, k, :],
                                         nodes[:, i, ds(n * BLK, w)], start=(i == 0), stop=(i == 1),
                                         skip_group_check=True)
                last.then_inc(ms["gmm"], 1)
                if more:
                    more([1, 2, 3, 4, 5])
                pe.wait_ge(ms["hn"], n + 1)
                for i in range(2):
                    last = pe.matmul(ps[:, 2, 0:w], m1[:, i, :], cc[:, 2, i, 0:w], start=(i == 0), stop=(i == 1),
                                     skip_group_check=True)
                last.then_inc(ms["w1"], 1)
                if more:
                    more([6, 7, 8])
                pe.wait_ge(ms["a1"], n + 1)
                pe.matmul(ps[:, 2, BLK:BLK + w], m2, mm1[:, 0:w], start=True, stop=True,
                          skip_group_check=True).then_inc(ms["w2"], 1)
                if more:
                    more([9, 10, 11, 12])
                pe.wait_ge(ms["a2"], n + 1)
                for a, (row, k) in enumerate(pieces(w)):
                    last = pe.matmul(ps[0:k, 6, a * D:(a + 1) * D], mm2[:, row:row + k], m3, start=True, stop=True,
                                     skip_group_check=True)
                last.then_inc(ms["w3"], 1)

            def general1():
                sum_all(1)
                pe.wait_ge(g_add, 2 * T * G)
                with pe.Fori(0, RUNS - 1) as n:
                    dense1(n, BLK, None, None, None)
                dense1(RUNS - 1, LAST, None, None, None)

            branch(pe, general1, lambda: edge_loop(1, dense1))

        @block.scalar
        def _(act):
            act.dma_start(raw_idx[:, :], edges[:, 0, 0, :]).then_inc(r_idx, 16)
            act.dma_start(early_sb[:, :], early).then_inc(s_par, 16)
            act.wait_ge(s_const, 1)

            def spread(k, var, done, count, tiles=slice(0, TB), lm=lm):
                act.wait_ge(var, count)
                act.activation(lm[:, k, 3, tiles], lm[:, k, 2, tiles], ACT.Sqrt, bias=epsc[:, 0:1]).then_inc(done, 1)

            def normal0(b, tiles):
                for t in tiles:
                    act.activation(h0[:, b * TB + t, :], xh[:, b * TB + t, :], ACT.Relu,
                                   bias=lm[:, b, 5, t:t + 1], scale=lm[:, b, 4, t:t + 1]).then_inc(s_h0, 1)

            spread(0, s_var, s_std, 1)
            for b in range(NB):
                act.wait_ge(s_rstd, b + 1)
                normal0(b, [0, 1, 2])
                if b + 1 < NB:
                    spread(b + 1, s_var, s_std, b + 2)
                normal0(b, [3, 4])
            spread(0, r_var, r_std, 1, slice(0, CH), raw_lm)
            act.wait_ge(r_rstd, 1)
            for c in range(CH):
                act.activation(msg[:, c, :], msg[:, c, :], ACT.Relu, bias=raw_lm[:, 0, 5, c:c + 1],
                               scale=raw_lm[:, 0, 4, c:c + 1]).then_inc(r_norm, 1)
            act.wait_ge(s_par, 16)
            for t in range(T):
                act.wait_ge(s_tr, t + 1)
                act.activation(h0t[:, :, t * P:(t + 1) * P],
                               ps[:, (3, 4, 6, 7)[t % 4], 0:2 * P].rearrange("p (h n) -> p h n", h=2), ACT.Copy,
                               scale=col("eps")[:, 0:1]).then_inc(s_h0t, 1)

            def z_act(n, w):
                act.wait_ge(zs["degm"], n + 1)
                act.activation(deg[:, ds(n * BLK, w)], deg[:, ds(n * BLK, w)], ACT.Sqrt).then_inc(zs["degs"], 1)
                act.wait_ge(zs["mm"], n + 1)
                act.activation(nodes[:, :, ds(n * BLK, w)],
                               ps[:, 2, 0:2 * BLK].rearrange("p (h n) -> p h n", h=2)[:, :, 0:w],
                               ACT.Copy).then_inc(zs["cp"], 1)

            with act.Fori(0, RUNS - 1) as n:
                z_act(n, BLK)
            z_act(RUNS - 1, LAST)


            def bn_std(k):
                act.wait_ge(s_bnv[k], 1)
                act.activation(bns[:, k, 0, :], bnv[:, k, :, 1], ACT.Sqrt, bias=epsc[:, 0:1]).then_inc(s_bnd[k], 1)

            act.wait_ge(s_late, 16)
            bn_std(0)
            act.wait_ge(s_bn[0], 1)

            def relu_z(n, w):
                for h in range(2):
                    last = act.activation(nodes[:, h, ds(n * BLK, w)], nodes[:, h, ds(n * BLK, w)], ACT.Relu,
                                          bias=bns[:, 0, 3, h:h + 1], scale=bns[:, 0, 2, h:h + 1])
                last.then_inc(s_hr, 1)

            with act.Fori(0, RUNS - 1) as n:
                relu_z(n, BLK)
            relu_z(RUNS - 1, LAST)
            bn_std(1)
            act.wait_ge(s_bn[1], 1)

            def relu_y(b, part=None):
                lo, hi = (q * P for q in tiles_of(part))
                if part is None:
                    act.wait_ge(s_ta, signals(b - 1, None))
                for h in range(2):
                    last = act.activation(r_sb[:, h, lo:hi], nodes[:, h, ds(b * BN + lo, hi - lo)], ACT.Relu,
                                          bias=bns[:, 1, 3, h:h + 1], scale=bns[:, 1, 2, h:h + 1])
                last.then_inc(s_r, 1)

            def spread1(b, part=None):
                n = signals(b, part)
                spread(0, s_var1, s_std1, n, slice(*tiles_of(part)))

            def normal1(b, tiles, first, last, part=None):
                if first:
                    act.wait_ge(s_rstd1, signals(b, part))
                    if part is None:
                        act.wait_ge(s_tb, signals(b - 1, None))
                for t in tiles:
                    done = act.activation(h1[:, t, :], xh[:, ds(b * TB + t, 1), :].rearrange("p a d -> p (a d)"),
                                          ACT.Relu, bias=lm[:, 0, 5, t:t + 1], scale=lm[:, 0, 4, t:t + 1])
                if last:
                    done.then_inc(s_h1, 1)

            def features_upper(b):
                act.wait_ge(s_tb, signals(b, None))
                for t, k, bank in banks:
                    act.activation(in_tiles(h1t_up, t, k), in_bank(bank, k), ACT.Copy).then_inc(s_h1u, 1)

            def hidden(b, ks):
                for k in ks:
                    (lo, hi), r, o = CHUNKS[k // 4], k // 2 % 2, k % 2
                    act.wait_ge(s_l1, b * 8 + k + 1)
                    act.activation(hid[:, r, o, lo:hi], ps[:, 6 + k % 2, 0:hi - lo],
                                   ACT.Relu, bias=brel[:, r, o:o + 1]).then_inc(s_hid, 1)

            def message_relu(b, tiles):
                for t in tiles:
                    act.wait_ge(s_l2a, b * TB + t + 2)
                    act.activation(mst[:, t, :, :], mst[:, t, :, :], ACT.Relu).then_inc(s_m, 1)

            for part in range(2):
                relu_y(0, part)
            for part in range(2):
                spread1(0, part)
                normal1(0, range(*PARTS[part]), True, True, part)
            relu_y(1)
            hidden(0, [0, 1, 2, 3])

            def message_turn(b, ahead):
                hidden(b, [4, 5])
                spread1(b + 1)
                hidden(b, [6])
                normal1(b + 1, [0], True, False)
                hidden(b, [7])
                normal1(b + 1, [1, 2, 3, 4], False, True)
                message_relu(b, [0, 1])
                features_upper(b + 1)
                if ahead:
                    relu_y(b + 2)
                message_relu(b, [2, 3])
                hidden(b + 1, [0])
                message_relu(b, [4])
                hidden(b + 1, [1, 2, 3])

            with act.Fori(0, NB - 2) as b:
                message_turn(b, True)
            message_turn(NB - 2, False)
            hidden(NB - 1, [4, 5, 6, 7])
            message_relu(NB - 1, range(TB))

            def mlp_act(n, w):
                act.wait_ge(ms["gmm"], n + 1)
                for k in range(6):
                    last = act.activation(gat[:, k, 0:w], ps[:, 3 + k // 2, (k % 2) * BLK:(k % 2) * BLK + w],
                                          ACT.Tanh if k in (2, 3) else ACT.Sigmoid, bias=bg[:, k:k + 1])
                last.then_inc(ms["gact"], 1)
                act.wait_ge(ms["c"], n + 1)
                act.activation(cc[:, 1, :, 0:w], cc[:, 0, :, 0:w], ACT.Tanh).then_inc(ms["tc"], 1)
                act.wait_ge(ms["w1"], n + 1)
                act.activation(mm1[:, 0:w], ps[:, 2, 0:w], ACT.Relu, bias=col("b1")).then_inc(ms["a1"], 1)
                act.wait_ge(ms["w2"], n + 1)
                act.activation(mm2[:, 0:w], ps[:, 2, BLK:BLK + w], ACT.Relu, bias=col("b2")).then_inc(ms["a2"], 1)

            with act.Fori(0, RUNS - 1) as n:
                mlp_act(n, BLK)
            mlp_act(RUNS - 1, LAST)

        @block.vector
        def _(dve):
            own = Steps(dve, s_dve)
            free_at_first(dve, s_mtab, ms["st0"])
            free_at_first(dve, s_oh[0], s_oh[1])
            def row_moments(k, var, tiles=slice(0, TB), lst=lst, lm=lm):
                me, mo, ve, vo = (lst[:, k, tiles, q] for q in (1, 4, 2, 5))
                own.sync()
                dve.tensor_tensor(lm[:, k, 0, tiles], me, mo, ALU.add)
                dve.tensor_tensor(lm[:, k, 1, tiles], me, mo, ALU.subtract)
                own.mark(dve.tensor_tensor(lm[:, k, 2, tiles], ve, vo, ALU.add))
                own.sync()
                dve.tensor_scalar(lm[:, k, 0:2, tiles], lm[:, k, 0:2, tiles], 0.5, None, ALU.mult)
                own.mark(dve.tensor_scalar(lm[:, k, 2, tiles], lm[:, k, 2, tiles], 1.0 / D, None, ALU.mult))
                own.sync()
                own.mark(dve.tensor_tensor(lm[:, k, 1, tiles], lm[:, k, 1, tiles], lm[:, k, 1, tiles], ALU.mult))
                own.sync()
                dve.tensor_tensor(lm[:, k, 2, tiles], lm[:, k, 2, tiles], lm[:, k, 1, tiles], ALU.add
                                  ).then_inc(var, 1)

            def row_scales(k, std, count, done, tiles=slice(0, TB), lm=lm):
                dve.wait_ge(std, count)
                own.mark(dve.reciprocal(lm[:, k, 4, tiles], lm[:, k, 3, tiles]))
                own.sync()
                dve.scalar_tensor_tensor(out=lm[:, k, 5, tiles], in0=lm[:, k, 0, tiles], scalar=-1.0,
                                         in1=lm[:, k, 4, tiles], op0=ALU.mult, op1=ALU.mult).then_inc(done, 1)

            for b in range(NB):
                dve.wait_ge(s_xin[b], 16)
                for t in range(TB):
                    last = dve.bn_stats(lst[:, b, t, :], xh[:, b * TB + t, :])
                own.mark(last)
                if b >= 1:
                    row_scales(b - 1, s_std, b, s_rstd)
                row_moments(b, s_var)
            dve.wait_ge(s_edge, 48)
            dve.scalar_tensor_tensor(out=ed[:, :, 1, :], in0=ed[:, :, 1, :], scalar=float(NP), in1=ed[:, :, 0, :],
                                     op0=ALU.mult, op1=ALU.add)
            own.mark(dve.tensor_tensor(ed[:, :, 2, :].bitcast(F32), ed[:, :, 2, :],
                                       bi[:, :].rearrange("p (g o) -> p g o", o=1).broadcast_to([P, G, CH]),
                                       ALU.subtract))
            row_scales(NB - 1, s_std, NB, s_rstd)
            rel = ed[:, 0:G, 2, :].bitcast(F32)
            dve.wait_ge(s_par, 16)
            own.sync()
            t1 = tmp[:, :].rearrange("p (g c) -> p g c", g=G)
            t2 = tmp2[:, :].rearrange("p (g c) -> p g c", g=G)
            own.mark(dve.tensor_scalar(t1, rel, 0.0, None, ALU.is_lt))
            own.sync()
            own.mark(dve.scalar_tensor_tensor(out=t2, in0=rel, scalar=float(P - 1), in1=t1, op0=ALU.is_gt,
                                              op1=ALU.add))
            own.sync()
            dve.reduce_sum(cnt[:, 0:1], tmp2[:, :], axis=AX_X)
            own.mark(dve.tensor_tensor(tmp[:, 0:G], bi[:, 0:G], col("lim"), ALU.is_lt))
            own.sync()
            own.mark(dve.reduce_sum(cnt[:, 1:2], tmp[:, 0:G], axis=AX_X))
            own.sync()
            dve.tensor_tensor(cnt[:, 2:3], cnt[:, 0:1], cnt[:, 1:2], ALU.add).then_inc(s_cnt, 1)
            dve.wait_ge(s_cntp, 1)
            dve.tensor_scalar(badi[:, :], ps[0:1, 5, 0:1], -float(NPAD), None, ALU.add).then_inc(s_flag, 1)

            def indices(h, g, layer):
                if layer == 0:
                    dve.tensor_copy(stw[:, h, :], ew[:, ds(g, 1), :].rearrange("p a c -> p (a c)"))
                dve.tensor_copy(st[:, h, :, :], ed[:, ds(g, 1), :, :].rearrange("p a k c -> p (a k) c")
                                ).then_inc(s_st[h], 1)

            def places(h, turn, layer, first=False):
                dve.wait_ge(s_st[h], turn + 1)
                last = one_hots(h, layer, first)
                if not first:
                    last.then_inc(s_oh[h], 1)

            def stage(h, turn, g, layer):
                indices(h, g, layer)
                places(h, turn, layer)

            def normalise_raw():
                for c in range(CH):
                    dve.wait_ge(s_slot[c], 16)
                    last = dve.bn_stats(raw_st[:, 0, c, :], msg[:, c, :])
                own.mark(last)
                row_moments(0, r_var, slice(0, CH), raw_st, raw_lm)
                row_scales(0, r_std, 1, r_rstd, slice(0, CH), raw_lm)

            def one_hots(h, layer, each=False):
                rel = st[:, h, 2, :].bitcast(F32)
                for c in range(CH):
                    k = h * CH + c
                    if layer == 0:
                        dve.tensor_scalar(oh[:, k, :], iota[:, 0:P], rel[:, c:c + 1], stw[:, h, c:c + 1],
                                          ALU.is_equal, ALU.mult)
                        last = dve.tensor_scalar(ohb[:, k, :], iota[:, 0:P], rel[:, c:c + 1], None, ALU.is_equal)
                    else:
                        last = dve.tensor_scalar(oh[:, k, :], iota[:, 0:P], rel[:, c:c + 1], None, ALU.is_equal)
                    if each:
                        last.then_inc(r_oh, 1)
                return last

            def add(h, turn, g, layer):
                dve.wait_ge(s_sum[h], turn + 1)
                base = dve.value_load(bi[0:1, ds(g, 1)], min_val=0, max_val=N - 1)
                dve.wait_ge(s_add[1 - h], turn + h)
                if layer == 0:
                    dve.tensor_tensor(deg[:, ds(base, P)], deg[:, ds(base, P)], ps[:, h, 2 * P:3 * P], ALU.add)
                win = nodes[:, :, ds(base, P)]
                dve.tensor_tensor(win, win, ps[:, h, 0:2 * P].rearrange("p (h n) -> p h n", h=2), ALU.add
                                  ).then_inc(s_add[h], 1)

            def z_in(n, w, general=False):
                if general:
                    dve.wait_ge(g_add, T * G)
                elif w == BLK:
                    dve.wait_ge(s_add[0], n + 2)
                else:
                    dve.wait_ge(s_add[1], RUNS)
                dve.tensor_tensor(yb[:, :, 0:w], nodes[:, :, ds(n * BLK, w)], h0t[:, :, ds(n * BLK, w)],
                                  ALU.add).then_inc(zs["yb"], 1)
                d = deg[:, ds(n * BLK, w)]
                dve.tensor_scalar(d, d, 1.0, None, ALU.max).then_inc(zs["degm"], 1)

            def z_out(n, w, general=False):
                wait_alone(dve, zs["degs"], n + 1)
                d = deg[:, ds(n * BLK, w)]
                dve.reciprocal(d, d)
                wait_alone(dve, zs["cp"], n + 1)
                for h in range(2):
                    last = dve.bn_stats(zst[:, h, ds(n, 1), :].rearrange("p a s -> p (a s)"),
                                        nodes[:, h, ds(n * BLK, w)])
                last.then_inc(zs["st"], 1)

            def edge_loop(layer, before, after, per):
                o = layer * RUNS
                indices(0, 0, layer)
                indices(1, 1, layer)
                if layer == 0:
                    normalise_raw()
                dve.wait_ge(s_sums0, layer + 1)
                places(0, o, layer, layer == 0)
                add(0, o, 0, layer)
                indices(0, 2, layer)
                places(1, o, layer, layer == 0)
                add(1, o, 1, layer)
                indices(1, 3, layer)
                places(0, 1 + o, layer)
                places(1, 1 + o, layer)
                if layer == 0:
                    dve.wait_ge(s_h0t, T)
                add(0, 1 + o, 2, layer)
                stage(0, 2 + o, 4, layer)
                def turn(i):
                    before(i - 1, BLK)
                    add(1, i + o, i * 2 + 1, layer)
                    stage(1, i + o + 1, i * 2 + 3, layer)
                    after(i - 1, BLK)
                    add(0, i + o + 1, i * 2 + 2, layer)

                with dve.Fori(1, RUNS - 2) as i:
                    own.enter(i - 1, per)
                    turn(i)
                    stage(0, i + o + 2, i * 2 + 4, layer)
                    own.leave(RUNS - 3)
                turn(RUNS - 2)
                before(RUNS - 2, BLK)
                if layer == 0:
                    after(RUNS - 2, BLK)
                add(1, RUNS - 1 + o, G - 1, layer)
                if layer == 1:
                    after(RUNS - 2, BLK)
                before(RUNS - 1, LAST)
                after(RUNS - 1, LAST)

            def general(layer, before, after):
                at_branch = own.base, own.n
                if layer == 0:
                    normalise_raw()
                    dve.wait_ge(s_h0t, T)
                dve.wait_ge(s_sums0, layer + 1)
                dve.memset(woff[:, :], -float(P)).then_inc(g_off, 1)

                def window(w):
                    dve.wait_ge(g_off, w + layer * (T + 1) + 1)
                    dve.tensor_scalar(woff[:, :], woff[:, :], float(P), None, ALU.add).then_inc(g_off, 1)
                    wait_alone(dve, g_off, w + layer * (T + 1) + 2)

                def group(w, g, t):
                    dve.tensor_copy(stw[:, 0, :], ew[:, ds(g, 1), :].rearrange("p a c -> p (a c)"))
                    dve.scalar_tensor_tensor(
                        out=st[:, 0, 2, :].bitcast(F32),
                        in0=ed[:, ds(g, 1), 2, :].rearrange("p a c -> p (a c)").bitcast(F32), scalar=woff[:, 0:1],
                        in1=bi[:, ds(g, 1)].broadcast_to([P, CH]), op0=ALU.subtract, op1=ALU.add)
                    dve.tensor_copy(st[:, 0, 0:2, :], ed[:, ds(g, 1), 0:2, :].rearrange("p a k c -> p (a k) c")
                                    ).then_inc(g_st, 1)
                    dve.wait_ge(g_st, t + 1)
                    one_hots(0, layer).then_inc(g_oh, 1)
                    dve.wait_ge(g_sum, t + 1)
                    if layer == 0:
                        d = deg[:, ds(w * P, P)]
                        dve.tensor_tensor(d, d, ps[:, 0, 2 * P:3 * P], ALU.add)
                    win = nodes[:, :, ds(w * P, P)]
                    dve.tensor_tensor(win, win, ps[:, 0, 0:2 * P].rearrange("p (h n) -> p h n", h=2), ALU.add
                                      ).then_inc(g_add, 1)
                    wait_alone(dve, g_add, t + 1)

                windows(dve, layer, group, window)
                with dve.Fori(0, RUNS - 1) as n:
                    own.enter(n, layer)
                    before(n, BLK, True)
                    after(n, BLK, True)
                    own.leave(RUNS - 1)
                before(RUNS - 1, LAST, True)
                after(RUNS - 1, LAST, True)
                own.base, own.n = at_branch

            branch(dve, lambda: general(0, z_in, z_out), lambda: edge_loop(0, z_in, z_out, 0))
            dve.wait_ge(zs["st"], RUNS)

            dve.wait_ge(s_late, 16)

            def bn_scales(k, stats, gamma, beta):
                own.sync()
                for h in range(2):
                    last = dve.bn_aggr(bnv[:, k, h, :], stats[:, h, :, :].rearrange("p r s -> p (r s)"))
                last.then_inc(s_bnv[k], 1)
                dve.wait_ge(s_bnd[k], 1)
                own.mark(dve.reciprocal(bns[:, k, 1, :], bns[:, k, 0, :]))
                own.sync()
                own.mark(dve.tensor_tensor(bns[:, k, 2, :], bns[:, k, 1, :], gamma, ALU.mult))
                own.sync()
                own.mark(dve.tensor_tensor(bns[:, k, 1, :], bnv[:, k, :, 0], bns[:, k, 2, :], ALU.mult))
                own.sync()
                dve.tensor_tensor(bns[:, k, 3, :], beta, bns[:, k, 1, :], ALU.subtract).then_inc(s_bn[k], 1)

            dve.tensor_tensor(bg[:, :], col("bih"), col("bhh"), ALU.add)
            bn_scales(0, zst, col("g1"), col("be1"))

            def y_out(n, turn, k, w):
                dve.wait_ge(s_w2[k], turn + 1)
                both = ps[:, 6 + k, 0:2 * BLK].rearrange("p (h n) -> p h n", h=2)[:, :, 0:w]
                d = deg[:, ds(n * BLK, w)].rearrange("p (o n) -> p o n", o=1).broadcast_to([P, 2, w])
                dve.tensor_tensor(nodes[:, :, ds(n * BLK, w)], both, d, ALU.mult).then_inc(s_y[k], 1)

            def y_stats(n, turn, k, w):
                wait_alone(dve, s_y[k], turn + 2)
                for h in range(2):
                    last = dve.bn_stats(yst[:, h, ds(n, 1), :].rearrange("p a s -> p (a s)"),
                                        nodes[:, h, ds(n * BLK, w)])
                return last

            own.mark(dve.tensor_copy(wrel_up[:, :, :, :], wrel))
            own.sync()
            dve.tensor_tensor(wrel_lo[:, :, :, :], wrel, wrel_up[:, :, :, :].bitcast(F32), ALU.subtract
                              ).then_inc(s_wrel, 1)

            y_out(0, 0, 0, BLK)
            with dve.Fori(0, RUNS // 2 - 1) as j:
                for k in range(2):
                    y_out(j * 2 + k + 1, j + k, 1 - k, BLK)
                    y_stats(j * 2 + k, j, k, BLK)
            y_out(RUNS - 1, RUNS // 2 - 1, 1, LAST)
            y_stats(RUNS - 2, RUNS // 2 - 1, 0, BLK)
            own.mark(y_stats(RUNS - 1, RUNS // 2 - 1, 1, LAST))
            bn_scales(1, yst, col("gh"), col("beh"))

            def residual(b, part=None):
                n, tiles = signals(b, part), tiles_of(part)
                dve.wait_ge(s_xh, NB)
                dve.wait_ge(s_ta, n)
                for t, k, bank in banks_of(part):
                    rows = xh[:, ds(b * TB + t, k), :]
                    last = dve.tensor_tensor(rows, rows, ps[:, bank, 0:k * D].rearrange("p (t d) -> p t d", t=k),
                                             ALU.add)
                last.then_inc(s_x1, 1)
                dve.wait_ge(s_x1, n)
                if part is None:
                    wait_alone(dve, s_h1, signals(b - 1, None))
                for t in range(*tiles):
                    last = dve.bn_stats(lst[:, 0, t, :], xh[:, ds(b * TB + t, 1), :].rearrange("p a d -> p (a d)"))
                own.mark(last)
                row_moments(0, s_var1, slice(*tiles))

            def scales(b, part=None):
                row_scales(0, s_std1, signals(b, part), s_rstd1, slice(*tiles_of(part)))

            def features(b, part=None):
                if part is not None:
                    dve.wait_ge(s_tb, signals(b, part))
                    for t, k, bank in banks_of(part):
                        last = dve.tensor_copy(in_tiles(h1t_up, t, k), in_bank(bank, k))
                    own.mark(last)
                    own.sync()
                for n, (t, k, bank) in enumerate(banks_of(part)):
                    if part is None:
                        dve.wait_ge(s_h1u, (b - 1) * len(banks) + n + 1)
                    last = dve.tensor_tensor(in_tiles(h1t_lo, t, k), in_bank(bank, k),
                                             in_tiles(h1t_up, t, k).bitcast(F32), ALU.subtract)
                last.then_inc(s_h1t, 1)

            def message_bias(b, tiles):
                if tiles[0] == 0:
                    dve.wait_ge(s_mtab, b * 32 + 1)
                for t in tiles:
                    dve.wait_ge(s_l2, b * TB + t + 1)
                    dve.tensor_tensor(mst[:, t, :, :], ps[:, t % 2, :].rearrange("p (r d) -> p r d", r=2), brow,
                                      ALU.add).then_inc(s_l2a, 1)

            residual(0, 0)
            scales(0, 0)
            residual(0, 1)
            features(0, 0)
            scales(0, 1)
            features(0, 1)
            with dve.Fori(0, NB - 1) as b:
                own.enter(b, 5)
                residual(b + 1)
                scales(b + 1)
                message_bias(b, [0, 1, 2])
                features(b + 1)
                message_bias(b, [3, 4])
                own.leave(NB - 1)
            message_bias(NB - 1, list(range(TB)))

            def mlp_in(n, w, general=False):
                dve.wait_ge(ms["gact"], n + 1)
                dve.tensor_tensor(cc[:, 0, :, 0:w], gat[:, 0:2, 0:w], gat[:, 2:4, 0:w], ALU.mult
                                  ).then_inc(ms["c"], 1)
                dve.wait_ge(ms["tc"], n + 1)
                dve.tensor_tensor(cc[:, 2, :, 0:w], gat[:, 4:6, 0:w], cc[:, 1, :, 0:w], ALU.mult
                                  ).then_inc(ms["hn"], 1)

            def mlp_out(n, w, general=False):
                dve.wait_ge(ms["w3"], n + 1)
                dve.wait_ge(ms["xb"], n * 16 + 16)
                dve.wait_ge(ms["st0"], n * 16 + 1)
                b3 = col("b3")
                for a, (_, k) in enumerate(pieces(w)):
                    last = dve.tensor_tensor(ost[0:k, a, :], ps[0:k, 6, a * D:(a + 1) * D], b3[0:k, :], ALU.add)
                own.mark(last)
                own.sync()
                for a, (_, k) in enumerate(pieces(w)):
                    last = dve.tensor_tensor(ost[0:k, a, :], ost[0:k, a, :], xb[0:k, a, :], ALU.add)
                last.then_inc(ms["out"], 1)

            branch(dve, lambda: general(1, mlp_in, mlp_out), lambda: edge_loop(1, mlp_in, mlp_out, 1))


def kernel(**inputs):
    import concourse.bacc as _bacc
    from concourse.bass_utils import run_bass_kernel_spmd as _run

    g = {k: np.asarray(v) for k, v in inputs.items()}

    def chunks(a, fill):
        full = np.full(G * EG, fill, a.dtype)
        full[:E] = a
        return full.reshape(G, CH, P).transpose(2, 0, 1)

    edges = np.stack([chunks(g["src"], 0), chunks(g["edge_type_2"], 0), chunks(g["dst"], -1)], axis=2)
    firsts = np.zeros(G, np.int32)
    firsts[:G] = g["dst"][::EG]

    def halves(w):
        return np.ascontiguousarray(w.T).reshape(-1, P, w.shape[0]).transpose(1, 0, 2).reshape(P, -1)

    def cols(v):
        return v.reshape(-1, P).T

    used = [0, 1, 4, 5, 6, 7]
    wih = g["L1_gnn_W_ih"].reshape(8, P, D)[used].reshape(6 * P, D)
    params = {
        "w1": halves(g["L0_gnn_w1"]), "w2": halves(g["L0_gnn_w2"]),
        "wrel": np.concatenate([halves(g["L1_gnn_W_rel"][r]) for r in range(2)], axis=1),
        "wih": halves(wih), "m1": halves(g["L1_gnn_W1"]), "m2": halves(g["L1_gnn_W2"]), "m3": halves(g["L1_gnn_W3"]),
        "g1": cols(g["L0_gnn_gamma1"]), "be1": cols(g["L0_gnn_beta1"]),
        "gh": cols(g["L0_gnn_gamma_h"]), "beh": cols(g["L0_gnn_beta_h"]), "brel": cols(g["L1_gnn_b_rel"]),
        "bih": cols(g["L1_gnn_b_ih"])[:, used], "bhh": cols(g["L1_gnn_b_hh"])[:, used],
        "b1": cols(g["L1_gnn_b1"]), "b2": cols(g["L1_gnn_b2"]),
        "eps": np.broadcast_to(g["L0_gnn_eps_weight"][None], (P, 1)),
        "brow": np.broadcast_to(g["L1_gnn_b_rel"].reshape(1, -1), (P, 2 * D)),
        "b3": np.broadcast_to(g["L1_gnn_b3"][None], (P, D)),
        "ident": np.eye(P, dtype=np.float32),
        "iota": np.broadcast_to(np.arange(P, dtype=np.float32), (P, P)),
        "lim": np.broadcast_to(np.array([max(k - 1, 0) // 2 * BLK for k in range(G)], np.float32), (P, G)),
    }
    def packed(cols, n):
        a = np.zeros((P, n), np.float32)
        for name, (i, j) in cols.items():
            a[:, i:j] = params[name]
        return a

    x = np.zeros((NP, D), np.float32)
    x[:N] = g["x"]
    arrays = {
        "x": x,
        "edges": np.ascontiguousarray(edges.astype(np.int32)),
        "weights": np.ascontiguousarray(chunks(g["edge_weight"], 0)),
        "firsts": np.ascontiguousarray(np.broadcast_to(firsts, (P, G))),
        "early": packed(EARLY_COLS, NEARLY),
        "late": packed(LATE_COLS, NLATE),
    }
    nc = _bacc.Bacc("TRN2", target_bir_lowering=False, num_devices=1)
    args = [nc.dram_tensor("in_" + n, a.shape, mybir.dt.from_np(a.dtype), kind="ExternalInput").ap()
            for n, a in arrays.items()]
    out = nc.dram_tensor("out", (N, D), F32, kind="ExternalOutput").ap()
    build(nc, *args, out)
    r = _run(nc, [{"in_" + n: a for n, a in arrays.items()}], core_ids=[0])
    return r.results[0]["out"]
```
